# Optimizing a Trainium2 kernel written in Bass

```python
import numpy as np
import jax
import jax.numpy as jnp

def _softmax(x, axis=-1):
    return jax.nn.softmax(x, axis=axis)

def _gelu(x):
    return jax.nn.gelu(x, approximate=True)

def _silu(x):
    return jax.nn.silu(x)

def _sigmoid(x):
    return jax.nn.sigmoid(x)

def _layernorm(x, axis=-1, eps=1e-05):
    m = jnp.mean(x, axis=axis, keepdims=True)
    v = jnp.var(x, axis=axis, keepdims=True)
    return (x - m) / jnp.sqrt(v + eps)

def _scatter_add(tgt, idx, src, axis=0):
    return tgt.at[idx].add(src)

def _segment_sum(src, seg, n):
    return jax.ops.segment_sum(src, seg, n)
kernel_name = 'mk_adj_seq_d4_adj_r2_a27a22'

def setup_inputs(seed: int=0):
    np.random.seed(seed)
    _w = jnp.asarray

    def _rec_inputs():
        import jax
        import jax.numpy as jnp
        _gk = jax.random.key(seed)
        x = 7.22e-05 + 1 * jax.random.normal(jax.random.fold_in(_gk, 1), (128, 128, 256), jnp.float32)
        _w = (1.0 + jnp.arange(128, dtype=jnp.float32)) ** (-0.5)
        _w = _w / _w.mean()
        _pij = jnp.clip(0.03125 * _w[:, None] * _w[None, :], 0.0, 1.0)
        _a = jax.random.uniform(jax.random.fold_in(_gk, 2), (128, 128, 128)) < _pij
        _a = jnp.logical_or(_a, jnp.eye(128, dtype=bool))
        _af = _a.astype(jnp.float32)
        adj = _af
        return (x, adj)
    x, adj = _rec_inputs()

    def _L0_gnn_setup():
        import jax, jax.numpy as jnp
        import numpy as np
        BS, N, H = (8, 1024, 256)
        NEG_INF = -1000000000.0
        LEAKY_SLOPE = 0.01
        key = jax.random.key(seed)
        ks = jax.random.split(key, 8)
        feats = jax.random.normal(ks[0], (BS, N, H), dtype=jnp.float32)
        adj = jax.random.randint(ks[1], (BS, N, N), 0, 2).astype(jnp.float32)
        adj = jnp.maximum(adj, jnp.eye(N, dtype=jnp.float32)[None])
        s = 1.0 / np.sqrt(H)
        return {'feats': feats, 'adj_mat': adj, 'fc_w': jax.random.normal(ks[2], (H, H), dtype=jnp.float32) * s, 'fc_b': jax.random.normal(ks[3], (H,), dtype=jnp.float32) * s, 'q_w': jax.random.normal(ks[4], (1, H), dtype=jnp.float32) * s, 'q_b': jax.random.normal(ks[5], (1,), dtype=jnp.float32) * s, 'k_w': jax.random.normal(ks[6], (1, H), dtype=jnp.float32) * s, 'k_b': jax.random.normal(ks[7], (1,), dtype=jnp.float32) * s}
    _L0_gnn_all = _L0_gnn_setup()
    _L0_gnn_in = {k: v for k, v in _L0_gnn_all.items() if k in ('fc_w', 'fc_b', 'q_w', 'q_b', 'k_w', 'k_b')}
    del _L0_gnn_all

    def _L1_gnn_setup():
        import jax, jax.numpy as jnp
        import numpy as np
        import math
        EMBED = 256
        DFF = 256
        B, N = (8, 1024)
        key = jax.random.key(seed)
        ks = jax.random.split(key, 8)
        node_fts = jax.random.normal(ks[0], (B, N, EMBED), dtype=jnp.float32)
        rel_edges = jax.random.randint(ks[1], (B, N, N), 0, 2).astype(jnp.float32)
        s = 1.0 / math.sqrt(EMBED)
        Wq = jax.random.normal(ks[2], (EMBED, DFF), dtype=jnp.float32) * s
        bq = jnp.zeros((DFF,), dtype=jnp.float32)
        Wk = jax.random.normal(ks[3], (EMBED, DFF), dtype=jnp.float32) * s
        bk = jnp.zeros((DFF,), dtype=jnp.float32)
        Wc = jax.random.normal(ks[4], (EMBED, EMBED), dtype=jnp.float32) * s
        gamma = jnp.ones((EMBED,), dtype=jnp.float32)
        beta = jnp.zeros((EMBED,), dtype=jnp.float32)
        return {'node_fts': node_fts, 'rel_edges': rel_edges, 'Wq': Wq, 'bq': bq, 'Wk': Wk, 'bk': bk, 'Wc': Wc, 'gamma': gamma, 'beta': beta}
    _L1_gnn_all = _L1_gnn_setup()
    _L1_gnn_in = {k: v for k, v in _L1_gnn_all.items() if k in ('Wq', 'bq', 'Wk', 'bk', 'Wc', 'gamma', 'beta')}
    del _L1_gnn_all

    def _L2_gnn_setup():
        import jax, jax.numpy as jnp
        import numpy as np
        NUM_HEADS = 8
        EPS = 1e-09
        key = jax.random.key(seed)
        ks = jax.random.split(key, 8)
        B, N, D = (2, 1024, 256)
        s = 1.0 / np.sqrt(D)
        x = jax.random.normal(ks[0], (B, N, D), dtype=jnp.float32)
        adjacency = jax.random.uniform(ks[1], (B, N, N), dtype=jnp.float32)
        W_q = jax.random.normal(ks[2], (D, D), dtype=jnp.float32) * s
        W_k = jax.random.normal(ks[3], (D, D), dtype=jnp.float32) * s
        W_v = jax.random.normal(ks[4], (D, D), dtype=jnp.float32) * s
        b_q = jnp.zeros((D,), jnp.float32)
        b_k = jnp.zeros((D,), jnp.float32)
        b_v = jnp.zeros((D,), jnp.float32)
        w_g = jax.random.normal(ks[5], (2 * D,), dtype=jnp.float32) * (1.0 / np.sqrt(2 * D))
        b_g = jnp.zeros((), jnp.float32)
        return {'x': x, 'adjacency': adjacency, 'W_q': W_q, 'b_q': b_q, 'W_k': W_k, 'b_k': b_k, 'W_v': W_v, 'b_v': b_v, 'w_g': w_g, 'b_g': b_g}
    _L2_gnn_all = _L2_gnn_setup()
    _L2_gnn_in = {k: v for k, v in _L2_gnn_all.items() if k in ('W_q', 'b_q', 'W_k', 'b_k', 'W_v', 'b_v', 'w_g', 'b_g')}
    del _L2_gnn_all

    def _L3_gnn_setup():
        import jax, jax.numpy as jnp
        import numpy as np
        NUM_HID = 256
        BS, N = (8, 1024)
        NEG_BIG = -1000000000.0
        LEAKY_SLOPE = 0.01
        key = jax.random.key(seed)
        k_feats, k_adj, k_w, k_wq, k_wk = jax.random.split(key, 5)
        feats = jax.random.normal(k_feats, (BS, N, NUM_HID), dtype=jnp.float32)
        adj = (jax.random.uniform(k_adj, (BS, N, N)) < 0.05).astype(jnp.float32)
        eye = jnp.eye(N, dtype=jnp.float32)[None]
        adj_mat = jnp.maximum(adj, eye)
        s = 1.0 / np.sqrt(NUM_HID)
        W_fc = jax.random.uniform(k_w, (NUM_HID, NUM_HID), minval=-s, maxval=s, dtype=jnp.float32)
        b_fc = jnp.zeros((NUM_HID,), dtype=jnp.float32)
        w_q = jax.random.uniform(k_wq, (NUM_HID, 1), minval=-s, maxval=s, dtype=jnp.float32)
        b_q = jnp.zeros((1,), dtype=jnp.float32)
        w_k = jax.random.uniform(k_wk, (NUM_HID, 1), minval=-s, maxval=s, dtype=jnp.float32)
        b_k = jnp.zeros((1,), dtype=jnp.float32)
        return {'feats': feats, 'adj_mat': adj_mat, 'W_fc': W_fc, 'b_fc': b_fc, 'w_q': w_q, 'b_q': b_q, 'w_k': w_k, 'b_k': b_k}
    _L3_gnn_all = _L3_gnn_setup()
    _L3_gnn_in = {k: v for k, v in _L3_gnn_all.items() if k in ('W_fc', 'b_fc', 'w_q', 'b_q', 'w_k', 'b_k')}
    del _L3_gnn_all
    return {'x': x, 'adj': adj, 'L0_gnn_fc_w': _L0_gnn_in['fc_w'], 'L0_gnn_fc_b': _L0_gnn_in['fc_b'], 'L0_gnn_q_w': _L0_gnn_in['q_w'], 'L0_gnn_q_b': _L0_gnn_in['q_b'], 'L0_gnn_k_w': _L0_gnn_in['k_w'], 'L0_gnn_k_b': _L0_gnn_in['k_b'], 'L1_gnn_Wq': _L1_gnn_in['Wq'], 'L1_gnn_bq': _L1_gnn_in['bq'], 'L1_gnn_Wk': _L1_gnn_in['Wk'], 'L1_gnn_bk': _L1_gnn_in['bk'], 'L1_gnn_Wc': _L1_gnn_in['Wc'], 'L1_gnn_gamma': _L1_gnn_in['gamma'], 'L1_gnn_beta': _L1_gnn_in['beta'], 'L2_gnn_W_q': _L2_gnn_in['W_q'], 'L2_gnn_b_q': _L2_gnn_in['b_q'], 'L2_gnn_W_k': _L2_gnn_in['W_k'], 'L2_gnn_b_k': _L2_gnn_in['b_k'], 'L2_gnn_W_v': _L2_gnn_in['W_v'], 'L2_gnn_b_v': _L2_gnn_in['b_v'], 'L2_gnn_w_g': _L2_gnn_in['w_g'], 'L2_gnn_b_g': _L2_gnn_in['b_g'], 'L3_gnn_W_fc': _L3_gnn_in['W_fc'], 'L3_gnn_b_fc': _L3_gnn_in['b_fc'], 'L3_gnn_w_q': _L3_gnn_in['w_q'], 'L3_gnn_b_q': _L3_gnn_in['b_q'], 'L3_gnn_w_k': _L3_gnn_in['w_k'], 'L3_gnn_b_k': _L3_gnn_in['b_k']}

def reference(x, adj, L0_gnn_fc_w, L0_gnn_fc_b, L0_gnn_q_w, L0_gnn_q_b, L0_gnn_k_w, L0_gnn_k_b, L1_gnn_Wq, L1_gnn_bq, L1_gnn_Wk, L1_gnn_bk, L1_gnn_Wc, L1_gnn_gamma, L1_gnn_beta, L2_gnn_W_q, L2_gnn_b_q, L2_gnn_W_k, L2_gnn_b_k, L2_gnn_W_v, L2_gnn_b_v, L2_gnn_w_g, L2_gnn_b_g, L3_gnn_W_fc, L3_gnn_b_fc, L3_gnn_w_q, L3_gnn_b_q, L3_gnn_w_k, L3_gnn_b_k):
    import jax
    import jax.numpy as jnp

    def _L0_gnn_ref(feats, adj_mat, fc_w, fc_b, q_w, q_b, k_w, k_b):
        import jax, jax.numpy as jnp
        import numpy as np
        BS, N, H = (8, 1024, 256)
        NEG_INF = -1000000000.0
        LEAKY_SLOPE = 0.01
        feat_proj = jnp.einsum('bnh,oh->bno', feats, fc_w) + fc_b
        q = jnp.einsum('bnh,oh->bno', feat_proj, q_w) + q_b
        k = jnp.einsum('bnh,oh->bno', feat_proj, k_w) + k_b
        logits = q + jnp.swapaxes(k, 2, 1)
        masked = logits + (1.0 - adj_mat) * NEG_INF
        masked = jnp.where(masked >= 0, masked, LEAKY_SLOPE * masked)
        atten = jax.nn.softmax(masked, axis=-1)
        out = jnp.einsum('bnm,bmh->bnh', atten, feat_proj)
        return out + feats

    def _L1_gnn_ref(node_fts, rel_edges, Wq, bq, Wk, bk, Wc, gamma, beta):
        import jax, jax.numpy as jnp
        import numpy as np
        import math
        EMBED = 256
        DFF = 256
        B, N = (8, 1024)
        denom = math.sqrt(DFF)
        q = node_fts @ Wq + bq
        k = node_fts @ Wk + bk
        scores = jnp.einsum('bod,bid->boi', q, k) / denom
        mask = rel_edges == 0
        scores = jnp.where(mask, -1e+18, scores)
        attn = jax.nn.softmax(scores, axis=2)
        attn = jnp.where(mask, 0.0, attn)
        ctx = jnp.einsum('boi,bie->boe', attn, node_fts) @ Wc
        x = node_fts + ctx
        mu = jnp.mean(x, axis=-1, keepdims=True)
        var = jnp.mean(jnp.square(x - mu), axis=-1, keepdims=True)
        out = (x - mu) * jax.lax.rsqrt(var + 1e-05) * gamma + beta
        return out

    def _L2_gnn_ref(x, adjacency, W_q, b_q, W_k, b_k, W_v, b_v, w_g, b_g):
        import jax, jax.numpy as jnp
        import numpy as np
        NUM_HEADS = 8
        EPS = 1e-09
        B, N, D = x.shape
        H = NUM_HEADS
        hd = D // H
        Q = (x @ W_q + b_q).reshape(B, N, H, hd)
        K = (x @ W_k + b_k).reshape(B, N, H, hd)
        V = (x @ W_v + b_v).reshape(B, N, H, hd)
        scores = jnp.einsum('bihd,bjhd->bhij', Q, K) / jnp.sqrt(jnp.float32(hd))
        a = x @ w_g[:D]
        c = x @ w_g[D:]
        soul_bias = a[:, :, None] + c[:, None, :] + b_g
        scores = scores + (soul_bias + jnp.log(adjacency + EPS))[:, None, :, :]
        attn = jax.nn.softmax(scores, axis=-1)
        out = jnp.einsum('bhij,bjhd->bihd', attn, V).reshape(B, N, D)
        return out + x

    def _L3_gnn_ref(feats, adj_mat, W_fc, b_fc, w_q, b_q, w_k, b_k):
        import jax, jax.numpy as jnp
        import numpy as np
        NUM_HID = 256
        BS, N = (8, 1024)
        NEG_BIG = -1000000000.0
        LEAKY_SLOPE = 0.01
        feat_proj = jnp.einsum('bnd,de->bne', feats, W_fc) + b_fc
        q = jnp.einsum('bnd,do->bno', feat_proj, w_q) + b_q
        k = jnp.einsum('bnd,do->bno', feat_proj, w_k) + b_k
        logits = q + jnp.swapaxes(k, 2, 1)
        masked = logits + (1.0 - adj_mat) * NEG_BIG
        masked = jnp.where(masked >= 0, masked, LEAKY_SLOPE * masked)
        atten = jax.nn.softmax(masked, axis=-1)
        out = jnp.einsum('bnm,bmd->bnd', atten, feat_proj)
        return out + feats
    x = _L0_gnn_ref(x, adj, L0_gnn_fc_w, L0_gnn_fc_b, L0_gnn_q_w, L0_gnn_q_b, L0_gnn_k_w, L0_gnn_k_b)
    x = _L1_gnn_ref(x, adj, L1_gnn_Wq, L1_gnn_bq, L1_gnn_Wk, L1_gnn_bk, L1_gnn_Wc, L1_gnn_gamma, L1_gnn_beta)
    x = _L2_gnn_ref(x, adj, L2_gnn_W_q, L2_gnn_b_q, L2_gnn_W_k, L2_gnn_b_k, L2_gnn_W_v, L2_gnn_b_v, L2_gnn_w_g, L2_gnn_b_g)
    x = _L3_gnn_ref(x, adj, L3_gnn_W_fc, L3_gnn_b_fc, L3_gnn_w_q, L3_gnn_b_q, L3_gnn_w_k, L3_gnn_b_k)
    return x

_drawn_inputs = setup_inputs


def setup_inputs(seed=0):
    import zlib

    import numpy as np

    out = dict(_drawn_inputs(seed))
    spreads = {'L1_gnn_bq': (0.0, 0.285),
     'L1_gnn_bk': (0.0, 0.8),
     'L1_gnn_gamma': (1.0, 0.2),
     'L1_gnn_beta': (0.0, 0.1),
     'L2_gnn_b_q': (0.0, 0.357),
     'L2_gnn_b_k': (0.0, 0.8),
     'L2_gnn_b_v': (0.0, 0.1),
     'L3_gnn_b_fc': (0.0, 0.1)}
    factors = {}
    for name, (base, spread) in spreads.items():
        noise = np.random.default_rng([zlib.crc32(name.encode()), seed]).standard_normal(out[name].shape)
        drawn = base * np.exp(spread * noise) if base else spread * noise
        out[name] = jnp.asarray(drawn.astype(out[name].dtype))
    for name, factor in factors.items():
        out[name] = (out[name] * factor).astype(out[name].dtype)
    return out
```

```python
from contextlib import ExitStack

import concourse.bass as bass
from concourse import mybir

ALU = mybir.AluOpType
ACT = mybir.ActivationFunctionType
AX_X = mybir.AxisListType.X
F32 = mybir.dt.float32
F32R = mybir.dt.float32r

P = 128
G = 2
D = 256
C = D // P
H = 8
HD = D // H
QUADS = P // HD
DX = D + 2
NEG_LEAKY = -1.0e9
NEG_MASK = -1.0e18
SLOPE = 0.01
HUGE = 3.0e38
LN_EPS = 1e-5
ADJ_EPS = 1e-9

L0, L1, L2A, L2B, L3 = 0, 1, 2, 3, 4
LAST_LAG = L3
PEEL = 6

BANK_USERS = {
    0: [("sc0", L2B), ("sc2", L2B), ("pt2_0", L2B), ("pt2_2", L2B), ("cb2", L2A)],
    1: [("sc1", L2B), ("sc3", L2B), ("pt2_1", L2B), ("pt2_3", L2B), ("pt3", L3)],
    2: [("xt0", L0), ("tt1", L1), ("s1", L1), ("pt1", L1), ("pv3", L3)],
    3: [("xt1", L1), ("kb0", L0), ("kb3", L3), ("v2", L2A)],
    4: [("xt3", L3), ("xc1", L1), ("qt2", L2A), ("v2", L2A)],
    5: [("xt2", L2A), ("xc1", L1), ("pt0", L0), ("pv2_0", L2B)],
    6: [("p0", L0), ("p3", L3), ("kt2", L2A), ("pv1", L1)],
    7: [("p0", L0), ("p3", L3), ("pv0", L0), ("pv2_1", L2B)],
}
PRODUCTS = sorted({name for users in BANK_USERS.values() for name, _ in users})

SEMAPHORES = (
    "x_loaded0 x_loaded1 adj_loaded0 adj_loaded1 y_stored0 y_stored1 const_loaded prep_transposed prep_products prep_copied "
    "prep_columns prep_chain prep_done fills_done "
    "hi0 hi1 hi2 hi3 "
    "qk0 qk3 row1 ac2 leaky0 leaky3 max0 max1 max3 exp0 exp1 exp3 rinv0 rinv1 rinv3 xb0 xb3 xb2 "
    "full1 flag1 rflag1 stats1 mean1 veps1 rstd1 norm1 gamma1 x2_ready "
    "pair_bias2 exp2_0 exp2_1 exp2_2 exp2_3 rinv2_0 rinv2_1 x3_ready "
    "neg0 neg1 neg3 adj1"
).split()


def build_program(nc, ins, out):
    x_dram, adj_dram = ins["x"], ins["adj"]
    pairs = x_dram.shape[0] // G

    with ExitStack() as ctx:
        def sb(name, shape, dtype=F32):
            return ctx.enter_context(nc.sbuf_tensor(name, shape, dtype))

        s = {n: ctx.enter_context(nc.semaphore(n)) for n in SEMAPHORES}
        made = {n: ctx.enter_context(nc.semaphore(f"{n}_made")) for n in PRODUCTS}
        drained = {n: ctx.enter_context(nc.semaphore(f"{n}_drained")) for n in PRODUCTS}

        x_loaded, adj_loaded = (s["x_loaded0"], s["x_loaded1"]), (s["adj_loaded0"], s["adj_loaded1"])
        y_stored = (s["y_stored0"], s["y_stored1"])

        ps = ctx.enter_context(nc.psum_tensor("ps", [P, 8, 512], F32))

        ident = sb("ident", [P, P])
        wraw = {n: sb(f"raw_{n}", [P, C, D]) for n in ("fc0", "wq1", "wk1", "wfc3")}
        wtr = {n: sb(f"tr_{n}", [P, C, D]) for n in ("wq1", "wk1", "wfc3")}
        wide = {n: sb(f"w_{n}", [P, C, DX]) for n in ("0", "1c", "1m", "2q", "2k", "2v", "3")}
        whi = {n: sb(f"whi_{n}", [P, C, DX], F32R) for n in wide}
        wlo = {n: sb(f"wlo_{n}", [P, C, DX], F32R) for n in wide}
        rows = {n: sb(f"row_{n}", [P, D]) for n in
                ("fc_b0", "q_w0", "k_w0", "bq1", "bk1", "gamma", "beta", "bv2", "b_fc3", "w_q3", "w_k3")}
        one = {n: sb(f"one_{n}", [P, 1]) for n in ("q_b0", "k_b0", "b_g2", "b_q3", "b_k3")}
        cols = {n: sb(f"col_{n}", [P, C]) for n in
                ("q_w0", "k_w0", "bq1", "bk1", "bq2", "bk2", "w_q3", "w_k3")}
        qk_cols = {n: sb(f"qk_cols{n}", [P, C, 2]) for n in (0, 3)}
        scratch = sb("scratch", [P, 6, D])
        dots = sb("dots", [P, 8])
        qk_const = {n: sb(f"qk_const{n}", [P, G, 2]) for n in (0, 3)}
        row_const1 = sb("row_const1", [P, 1])
        tt_bias1 = sb("tt_bias1", [P, C])
        q_bias2 = sb("q_bias2", [P, C])
        minus_half = sb("minus_half", [P, G])

        x0, x1, x2b = (sb(n, [P, 2, G, D]) for n in ("x0", "x1", "x2b"))
        adj0, adj1 = sb("adj0", [P, 2, G, P]), sb("adj1", [P, 2, G, P])
        x2, x3, y = sb("x2", [P, G, D]), sb("x3", [P, G, D]), sb("y", [P, 2, G, D])
        neg = {0: sb("neg0_sb", [P, G, P]), 1: sb("neg1_sb", [P, G, P]), 3: sb("neg3_sb", [P, 2, G, P])}
        xhi = {n: sb(f"xhi{n}", [P, C, G, P], F32R) for n in range(4)}
        xlo = {n: sb(f"xlo{n}", [P, C, G, P], F32R) for n in range(4)}
        qk = {n: sb(f"qk_sb{n}", [P, G, 2]) for n in (0, 3)}
        fp = {n: sb(f"fp_sb{n}", [P, G, D]) for n in (0, 3)}
        xb = {n: sb(f"xb_sb{n}", [P, G, D]) for n in (0, 3)}
        lk = {n: sb(f"leaky_sb{n}", [P, G, P]) for n in (0, 3)}
        z = {n: sb(f"z_sb{n}", [P, G, P]) for n in (0, 1, 3)}
        nmax = {n: sb(f"nmax{n}", [P, G]) for n in (0, 1, 3)}
        e = {n: sb(f"e_sb{n}", [P, G, P]) for n in (0, 1, 3)}
        rsum = {n: sb(f"rsum{n}", [P, G]) for n in (0, 1, 3)}
        rinv = {n: sb(f"rinv_sb{n}", [P, G]) for n in (0, 1, 3)}
        pt = {n: sb(f"pt_sb{n}", [P, G, P]) for n in (0, 1, 3)}
        xt1 = sb("xt1_sb", [P, C, G, P])
        tt1 = sb("tt1_sb", [P, C, G, P])
        row1 = sb("row1_sb", [P, G])
        xc1 = sb("xc1_sb", [P, G, D])
        flag1, rflag1, veps1, rstd1 = (sb(f"{n}_sb", [P, G]) for n in ("flag1", "rflag1", "veps1", "rstd1"))
        sum1, norm1, gam1 = (sb(f"{n}_sb", [P, G, D]) for n in ("sum1", "norm1", "gam1"))
        stats1, mean1 = sb("stats1_sb", [P, G, 6]), sb("mean1_sb", [P, G, 2])
        qt2, kt2 = sb("qt2_sb", [P, C, G, P]), sb("kt2_sb", [P, C, G, P])
        ac2 = sb("ac2_sb", [P, G, 2])
        v2 = sb("v2_sb", [P, 2, G, H, HD + 1])
        pair_bias2, adjt2 = sb("pair_bias2_sb", [P, G, P]), sb("adjt2_sb", [P, G, P])
        t2, e2, ptm2 = (sb(n, [P, QUADS, C, G, P]) for n in ("t2_sb", "e2_sb", "ptm2_sb"))
        nmax2 = sb("nmax2", [P, QUADS, C, G])
        rinv2 = sb("rinv2_sb", [P, G, H])
        o2 = sb("o2_sb", [P, G, D])

        n_loads = [0]

        class Step:

            def __init__(self, t, count=None):
                self.t = t
                self.count = count
                self.even = None if count is None else count * 2

            def runs(self, lag):
                return self.even is not None or 0 <= self.t - lag < pairs

            def half(self, lag):
                return (self.t - lag) % 2

            def pair(self, lag):
                return self.t - lag if self.even is None else self.even + (self.t - lag)

            def turn(self, lag):
                return (self.t - lag) // 2 if self.count is None else self.count + (self.t - lag) // 2

        def moved(eng, sems, step, lag, before=0):
            if step.count is not None or step.turn(lag) - before >= 0:
                eng.wait_ge(sems[step.half(lag)], (step.turn(lag) + (1 - before)) * 16)

        def ready(eng, sem, step, lag):
            eng.wait_ge(sem, step.pair(lag) + 1)

        def read_out(eng, sem, step, lag, halves=1):
            if step.even is not None or step.pair(lag) + 1 - halves > 0:
                eng.wait_ge(sem, step.pair(lag) + (1 - halves))

        def take_bank(eng, bank, name, step):
            users = BANK_USERS[bank]
            at = [n for n, _ in users].index(name)
            before = users[:at][::-1]
            for back in range(LAST_LAG + 2):
                for who, lag in before:
                    if step.even is not None:
                        eng.wait_ge(drained[who], step.even + (step.t - back - lag + 1))
                        return
                    if 0 <= step.t - back - lag < pairs:
                        eng.wait_ge(drained[who], step.t - back - lag + 1)
                        return
                before = users[::-1]

        def after_setup(eng):
            eng.nop(nofuse=True)

        def pipeline(eng, one_step):
            for t in range(PEEL):
                one_step(Step(t))
            with eng.Fori(PEEL // 2, pairs // 2) as i:
                for u in range(2):
                    one_step(Step(u, i))
            for t in range(pairs, pairs + LAST_LAG):
                one_step(Step(t))

        def graphs(dram, pair):
            rows_ = slice(pair * G, (pair + 1) * G) if isinstance(pair, int) else bass.ds(pair * G, G)
            return dram[rows_].rearrange("g n d -> n g d")

        def flat(ap):
            return ap.rearrange("p a b -> p (a b)")

        block = ctx.enter_context(nc.Block())

        @block.sync
        def _(sp):
            def load(dst, src):
                n_loads[0] += 1
                sp.dma_start(dst, src).then_inc(s["const_loaded"], 16)

            def load_x(pair, half):
                sp.dma_start(x0[:, half], graphs(x_dram, pair)).then_inc(x_loaded[half], 16)

            def load_adj(pair, half):
                sp.dma_start(adj0[:, half], graphs(adj_dram, pair)).then_inc(adj_loaded[half], 16)

            load(ident[:], ins["ident"])
            for n, src in (("fc0", "L0_gnn_fc_w"), ("wfc3", "L3_gnn_W_fc"), ("wq1", "L1_gnn_Wq"), ("wk1", "L1_gnn_Wk")):
                load(wraw[n][:], ins[src].rearrange("(c p) n -> p c n", p=P))
            for n, src in (("1c", "L1_gnn_Wc"), ("2q", "L2_gnn_W_q"), ("2k", "L2_gnn_W_k"), ("2v", "L2_gnn_W_v"),
                           ("3", "L3_gnn_W_fc")):
                load(wide[n][:, :, 0:D], ins[src].rearrange("(c p) n -> p c n", p=P))
            for n, src in (("fc_b0", "L0_gnn_fc_b"), ("q_w0", "L0_gnn_q_w"), ("k_w0", "L0_gnn_k_w"),
                           ("bq1", "L1_gnn_bq"), ("bk1", "L1_gnn_bk"), ("gamma", "L1_gnn_gamma"),
                           ("beta", "L1_gnn_beta"), ("bv2", "L2_gnn_b_v"), ("b_fc3", "L3_gnn_b_fc"),
                           ("w_q3", "L3_gnn_w_q"), ("w_k3", "L3_gnn_w_k")):
                load(rows[n][:], ins[src].rearrange("(o d) -> o d", o=1).broadcast_to([P, D]))
            for n, src in (("q_b0", "L0_gnn_q_b"), ("k_b0", "L0_gnn_k_b"), ("b_g2", "L2_gnn_b_g"),
                           ("b_q3", "L3_gnn_b_q"), ("b_k3", "L3_gnn_b_k")):
                load(one[n][:], ins[src].rearrange("(o d) -> o d", o=1).broadcast_to([P, 1]))
            with nc.allow_non_contiguous_dma(reason="vectors of 256 words onto partitions, once"):
                for n, src in (("q_w0", "L0_gnn_q_w"), ("k_w0", "L0_gnn_k_w"), ("bq1", "L1_gnn_bq"),
                               ("bk1", "L1_gnn_bk"), ("bq2", "L2_gnn_b_q"), ("bk2", "L2_gnn_b_k"),
                               ("w_q3", "L3_gnn_w_q"), ("w_k3", "L3_gnn_w_k")):
                    load(cols[n][:], ins[src].rearrange("(c p) -> p c", p=P))
                for k in range(2):
                    load(wide["2v"][:, :, D + k],
                         ins["L2_gnn_w_g"][k * D:(k + 1) * D].rearrange("(c p) -> p c", p=P))
            for pair in range(2):
                load_x(pair, pair)
                load_adj(pair, pair)

            def one_step(step):
                if step.even is not None or step.t + 2 < pairs:
                    ready(sp, made["xt0"], step, L0)
                    ready(sp, s["xb0"], step, L0)
                    load_x(step.pair(L0 - 2), step.half(L0))
                if step.runs(L1) and (step.even is not None or step.t + 1 < pairs):
                    ready(sp, s["neg1"], step, L1)
                    ready(sp, s["adj1"], step, L1)
                    load_adj(step.pair(L0 - 1), step.half(L1))
                if step.runs(L3):
                    ready(sp, drained["pv3"], step, L3)
                    sp.dma_start(graphs(out, step.pair(L3)), y[:, step.half(L3)])\
                      .then_inc(y_stored[step.half(L3)], 16)

            for t in range(PEEL):
                one_step(Step(t))
            with sp.Fori(PEEL // 2, pairs // 2 - 1) as i:
                for u in range(2):
                    one_step(Step(u, i))
            for t in range(pairs - 2, pairs + LAST_LAG):
                one_step(Step(t))
            for half in range(2):
                sp.wait_ge(y_stored[half], 16 * pairs // 2)

        @block.tensor
        def _(pe):
            def transposes(bank, out_cols, src, step_end=None):
                last = None
                for dst, part in zip(out_cols, src):
                    last = pe.transpose(ps[:, bank, dst:dst + P], part, ident[:])
                return last

            pe.wait_ge(s["const_loaded"], 16 * n_loads[0])
            for bank, n in enumerate(("fc0", "wq1", "wk1", "wfc3")):
                for c in range(C):
                    last = transposes(bank, [cc * D + c * P for cc in range(C)],
                                      [wraw[n][:, c, cc * P:(cc + 1) * P] for cc in range(C)])
                last.then_inc(s["prep_transposed"], 1)
            pe.wait_ge(s["prep_copied"], 4)
            pe.wait_ge(s["prep_columns"], 1)

            def small(col, weight, vector, width):
                last = None
                for c in range(C):
                    for k in range(C):
                        last = pe.matmul(ps[:, 4, col + c * width:col + (c + 1) * width],
                                         weight[:, k, c * P:(c + 1) * P], vector[:, k],
                                         start=(k == 0), stop=(k == C - 1))
                return last

            small(0, wraw["fc0"], qk_cols[0], 2)
            small(4, wtr["wfc3"], qk_cols[3], 2)
            small(8, wtr["wk1"], cols["bq1"][:].rearrange("p (c o) -> p c o", o=1), 1)
            small(10, wtr["wq1"], cols["bk1"][:].rearrange("p (c o) -> p c o", o=1), 1).then_inc(s["prep_products"], 1)
            for c in range(C):
                for k in range(C):
                    last = pe.matmul(ps[:, 5, c * D:(c + 1) * D], wtr["wq1"][:, k, c * P:(c + 1) * P],
                                     wtr["wk1"][:, k, :], start=(k == 0), stop=(k == C - 1))
            last.then_inc(s["prep_products"], 1)
            pe.wait_ge(s["prep_done"], 1)
            pe.wait_ge(s["fills_done"], 1)

            def split_products(dst, left, right):
                terms = [(a, b, c) for a, b in ((0, 0), (0, 1), (1, 0)) for c in range(C)]
                for n, (a, b, c) in enumerate(terms):
                    last = pe.matmul(dst, left(a, c), right(b, c), start=(n == 0), stop=(n == len(terms) - 1))
                return last

            def x_transposes(n, bank, src, step, lag, sem=None):
                if not step.runs(lag):
                    return
                if n == 0:
                    moved(pe, x_loaded, step, lag)
                else:
                    ready(pe, sem, step, lag)
                take_bank(pe, bank, f"xt{n}", step)
                for c in range(C):
                    for g in range(G):
                        last = pe.transpose(ps[:, bank, (c * G + g) * P:(c * G + g + 1) * P],
                                            src[:, g, c * P:(c + 1) * P], ident[:])
                last.then_inc(made[f"xt{n}"], 1)

            def node_projection(name, n, banks, weight, step, lag):
                if not step.runs(lag):
                    return
                ready(pe, drained[f"xt{n}"], step, lag)
                for g in range(G):
                    take_bank(pe, banks[g], name, step)
                for g in range(G):
                    last = split_products(
                        ps[:, banks[g], 0:DX],
                        lambda a, c: (xhi, xlo)[a][n][:, c, g, :],
                        lambda b, c: (whi, wlo)[b][weight][:, c, :])
                last.then_inc(made[name], 1)

            def feature_projection(name, n, bank, weight, step, lag):
                if not step.runs(lag):
                    return
                ready(pe, drained[f"xt{n}"], step, lag)
                take_bank(pe, bank, name, step)
                for m in range(C):
                    last = split_products(
                        ps[:, bank, m * G * P:(m + 1) * G * P],
                        lambda a, c: (whi, wlo)[a][weight][:, c, m * P:(m + 1) * P],
                        lambda b, c: flat((xhi, xlo)[b][n][:, c]))
                last.then_inc(made[name], 1)

            def key_rows(n, bank, step, lag):
                if not step.runs(lag):
                    return
                sem = s["qk0"] if n == 0 else s["qk3"]
                ready(pe, sem, step, lag)
                take_bank(pe, bank, f"kb{n}", step)
                for g in range(G):
                    last = pe.transpose(ps[:, bank, g * P:(g + 1) * P],
                                        qk[n][:, g, 1:2].broadcast_to([P, P]), ident[:])
                last.then_inc(made[f"kb{n}"], 1)

            def prob_transposes(n, bank, exp_done, step, lag):
                if not step.runs(lag):
                    return
                ready(pe, exp_done, step, lag)
                take_bank(pe, bank, f"pt{n}", step)
                for g in range(G):
                    last = pe.transpose(ps[:, bank, g * P:(g + 1) * P], e[n][:, g, :], ident[:])
                last.then_inc(made[f"pt{n}"], 1)

            def weighted_sum(n, bank, values, copied, step, lag):
                if not step.runs(lag):
                    return
                ready(pe, drained[f"pt{n}"], step, lag)
                ready(pe, copied, step, lag)
                take_bank(pe, bank, f"pv{n}", step)
                for g in range(G):
                    last = pe.matmul(ps[:, bank, g * D:(g + 1) * D], pt[n][:, g, :], values[:, g, :],
                                     start=True, stop=True)
                last.then_inc(made[f"pv{n}"], 1)

            def scores1(step):
                if not step.runs(L1):
                    return
                ready(pe, drained["tt1"], step, L1)
                ready(pe, s["full1"], step, L1)
                take_bank(pe, 2, "s1", step)
                for g in range(G):
                    for c in range(C):
                        last = pe.matmul(ps[:, 2, g * P:(g + 1) * P], tt1[:, c, g, :], xt1[:, c, g, :],
                                         start=(c == 0), stop=(c == C - 1))
                last.then_inc(made["s1"], 1)

            def scores2(j, step):
                if not step.runs(L2B):
                    return
                if j == 0:
                    ready(pe, drained["qt2"], step, L2B)
                    ready(pe, drained["kt2"], step, L2B)
                bank, rows_of = j % 2, slice(j * HD, (j + 1) * HD)
                take_bank(pe, bank, f"sc{j}", step)
                for c in range(C):
                    for g in range(G):
                        last = pe.matmul(ps[:, bank, (c * G + g) * P:(c * G + g + 1) * P],
                                         qt2[rows_of, c, g, :], kt2[rows_of, c, g, :], start=True, stop=True)
                last.then_inc(made[f"sc{j}"], 1)

            def prob_transposes2(j, step):
                if not step.runs(L2B):
                    return
                exp_done = (s["exp2_0"], s["exp2_1"], s["exp2_2"], s["exp2_3"])[j]
                ready(pe, exp_done, step, L2B)
                bank = j % 2
                take_bank(pe, bank, f"pt2_{j}", step)
                for c in range(C):
                    for g in range(G):
                        last = pe.transpose(ps[:, bank, (c * G + g) * P:(c * G + g + 1) * P],
                                            e2[:, j, c, g, :], ident[:])
                last.then_inc(made[f"pt2_{j}"], 1)

            def weighted_sum2(g, step):
                if not step.runs(L2B):
                    return
                bank = (5, 7)[g]
                if g == 0:
                    ready(pe, drained["v2"], step, L2B)
                    for j in range(QUADS):
                        ready(pe, drained[f"pt2_{j}"], step, L2B)
                take_bank(pe, bank, f"pv2_{g}", step)
                for h in range(H):
                    last = pe.matmul(ps[:, bank, h * (HD + 1):(h + 1) * (HD + 1)],
                                     ptm2[:, h % QUADS, h // QUADS, g, :], v2[:, step.half(L2B), g, h, :],
                                     start=True, stop=True)
                last.then_inc(made[f"pv2_{g}"], 1)

            def bias_and_adjacency2(step):
                if not step.runs(L2A):
                    return
                ready(pe, s["ac2"], step, L2A)
                ready(pe, s["adj1"], step, L2A)
                take_bank(pe, 0, "cb2", step)
                for g in range(G):
                    pe.transpose(ps[:, 0, g * P:(g + 1) * P], ac2[:, g, 1:2].broadcast_to([P, P]), ident[:])
                for g in range(G):
                    last = pe.transpose(ps[:, 0, (G + g) * P:(G + g + 1) * P],
                                        adj1[:, step.half(L2A), g, :], ident[:])
                last.then_inc(made["cb2"], 1)

            def one_step(step):
                scores2(0, step)
                x_transposes(0, 2, x0[:, step.half(L0)], step, L0)
                x_transposes(1, 3, x1[:, step.half(L1)], step, L1, drained["pv0"])
                scores2(1, step)
                x_transposes(3, 4, x3, step, L3, s["x3_ready"])
                x_transposes(2, 5, x2, step, L2A, s["x2_ready"])
                node_projection("p0", 0, (6, 7), "0", step, L0)
                scores2(2, step)
                feature_projection("tt1", 1, 2, "1m", step, L1)
                scores2(3, step)
                key_rows(0, 3, step, L0)
                node_projection("xc1", 1, (4, 5), "1c", step, L1)
                node_projection("p3", 3, (6, 7), "3", step, L3)
                prob_transposes2(0, step)
                scores1(step)
                prob_transposes2(1, step)
                key_rows(3, 3, step, L3)
                feature_projection("qt2", 2, 4, "2q", step, L2A)
                prob_transposes(0, 5, s["exp0"], step, L0)
                prob_transposes2(2, step)
                feature_projection("kt2", 2, 6, "2k", step, L2A)
                weighted_sum(0, 7, fp[0], drained["p0"], step, L0)
                prob_transposes2(3, step)
                prob_transposes(1, 2, s["exp1"], step, L1)
                node_projection("v2", 2, (3, 4), "2v", step, L2A)
                weighted_sum2(0, step)
                weighted_sum(1, 6, xc1, drained["xc1"], step, L1)
                weighted_sum2(1, step)
                bias_and_adjacency2(step)
                prob_transposes(3, 1, s["exp3"], step, L3)
                weighted_sum(3, 2, fp[3], drained["p3"], step, L3)

            pipeline(pe, one_step)

        @block.scalar
        def _(act):
            def hi_part(n, bank, step, lag, hi_done, last_reads):
                if not step.runs(lag):
                    return
                ready(act, made[f"xt{n}"], step, lag)
                for reader in last_reads:
                    read_out(act, reader, step, lag)
                act.activation(xhi[n][:].rearrange("p c g n -> p (c g n)"), ps[:, bank, :], ACT.Copy)\
                   .then_inc(hi_done, 1)

            def copy_projection(name, dst, banks, columns_read, step, lag, last_read):
                if not step.runs(lag):
                    return
                ready(act, columns_read, step, lag)
                read_out(act, last_read, step, lag)
                act.activation(dst, ps[:, banks[0]:banks[1] + 1, 0:D], ACT.Copy).then_inc(drained[name], 1)

            def exponentials(n, max_done, exp_done, step, lag):
                if not step.runs(lag):
                    return
                ready(act, max_done, step, lag)
                read_out(act, made[f"pt{n}"], step, lag)
                src = z[1] if n == 1 else lk[n]
                for g in range(G):
                    last = act.activation(e[n][:, g, :], src[:, g, :], ACT.Exp, bias=nmax[n][:, g:g + 1],
                                          accum_out=rsum[n][:, g:g + 1])
                last.then_inc(exp_done, 1)

            def copy_probs(n, bank, step, lag):
                if not step.runs(lag):
                    return
                ready(act, made[f"pt{n}"], step, lag)
                read_out(act, made[f"pv{n}"], step, lag)
                act.activation(flat(pt[n][:]), ps[:, bank, 0:G * P], ACT.Copy).then_inc(drained[f"pt{n}"], 1)

            def biased_copy(name, bank, dst, scale, bias, step, lag, readers):
                if not step.runs(lag):
                    return
                ready(act, made[name], step, lag)
                for reader, reader_lag in readers:
                    read_out(act, reader, step, lag)
                for c in range(C):
                    last = act.activation(flat(dst[:, c]), ps[:, bank, c * G * P:(c + 1) * G * P],
                                          ACT.Identity, bias=bias[:, c:c + 1], scale=scale)
                last.then_inc(drained[name], 1)

            def exponentials2(j, step):
                if not step.runs(L2B):
                    return
                ready(act, drained[f"sc{j}"], step, L2B)
                read_out(act, made[f"pt2_{j}"], step, L2B)
                for c in range(C):
                    for g in range(G):
                        last = act.activation(e2[:, j, c, g, :], t2[:, j, c, g, :], ACT.Exp, scale=-1.0,
                                              bias=nmax2[:, j, c, g:g + 1])
                last.then_inc((s["exp2_0"], s["exp2_1"], s["exp2_2"], s["exp2_3"])[j], 1)

            def copy_v2(step):
                if not step.runs(L2A):
                    return
                ready(act, s["ac2"], step, L2A)
                read_out(act, made["pv2_1"], step, L2A, halves=2)
                for g in range(G):
                    last = act.activation(v2[:, step.half(L2A), g, :, 0:HD],
                                          ps[:, 3 + g, 0:D].rearrange("p (h d) -> p h d", h=H), ACT.Copy)
                last.then_inc(drained["v2"], 1)

            def one_step(step):
                hi_part(0, 2, step, L0, s["hi0"], [made["p0"]])
                hi_part(1, 3, step, L1, s["hi1"], [made["xc1"], s["full1"]])
                exponentials2(0, step)
                hi_part(3, 4, step, L3, s["hi3"], [made["p3"]])
                hi_part(2, 5, step, L2A, s["hi2"], [made["v2"]])
                exponentials2(1, step)
                copy_projection("p0", fp[0][:], (6, 7), s["qk0"], step, L0, made["pv0"])
                exponentials2(2, step)
                biased_copy("tt1", 2, tt1, 1.0 / 16.0, tt_bias1, step, L1, [(made["s1"], L1)])
                exponentials2(3, step)
                exponentials(0, s["max0"], s["exp0"], step, L0)
                copy_projection("xc1", xc1[:], (4, 5), s["row1"], step, L1, made["pv1"])
                copy_projection("p3", fp[3][:], (6, 7), s["qk3"], step, L3, made["pv3"])
                exponentials(1, s["max1"], s["exp1"], step, L1)
                biased_copy("qt2", 4, qt2, HD ** -0.5, q_bias2, step, L2A, [(made["sc3"], L2B)])
                copy_probs(0, 5, step, L0)
                exponentials(3, s["max3"], s["exp3"], step, L3)
                biased_copy("kt2", 6, kt2, 1.0, cols["bk2"], step, L2A, [(made["sc3"], L2B)])
                copy_probs(1, 2, step, L1)
                copy_v2(step)
                copy_probs(3, 1, step, L3)

            act.wait_ge(s["prep_done"], 1)
            pipeline(act, one_step)

        @block.vector
        def _(dve):
            chain = [0]

            def link(ins_):
                chain[0] += 1
                ins_.then_inc(s["prep_chain"], 1)
                dve.wait_ge(s["prep_chain"], chain[0])

            dve.wait_ge(s["const_loaded"], 16 * n_loads[0])
            for n, q, k in ((0, "q_w0", "k_w0"), (3, "w_q3", "w_k3")):
                link(dve.tensor_copy(qk_cols[n][:, :, 0], cols[q][:]))
                link(dve.tensor_copy(qk_cols[n][:, :, 1], cols[k][:]))
            dve.memset(wide["1c"][:, :, D:DX], 0.0).then_inc(s["prep_columns"], 1)
            for bank, dst in enumerate((wide["0"][:, :, 0:D], wtr["wq1"][:], wtr["wk1"][:], wtr["wfc3"][:])):
                dve.wait_ge(s["prep_transposed"], bank + 1)
                dve.tensor_copy(dst, ps[:, bank, :].rearrange("p (c n) -> p c n", c=C)).then_inc(s["prep_copied"], 1)
            for at, (a, b) in enumerate((("fc_b0", "q_w0"), ("fc_b0", "k_w0"), ("b_fc3", "w_q3"),
                                         ("b_fc3", "w_k3"), ("bq1", "bk1"))):
                link(dve.tensor_tensor_reduce(scratch[:, at], rows[a][:], rows[b][:], 1.0, 0.0, ALU.mult, ALU.add,
                                              dots[:, at:at + 1]))
            for at, (n, column, extra) in enumerate(((0, 0, "q_b0"), (0, 1, "k_b0"), (3, 0, "b_q3"), (3, 1, "b_k3"))):
                for g in range(G):
                    link(dve.tensor_tensor(qk_const[n][:, g, column:column + 1], dots[:, at:at + 1],
                                           one[extra][:], ALU.add))
            link(dve.tensor_scalar(row_const1[:], dots[:, 4:5], D ** -0.5, None, ALU.mult))
            link(dve.tensor_scalar(q_bias2[:], cols["bq2"][:], HD ** -0.5, None, ALU.mult))
            dve.wait_ge(s["prep_products"], 1)
            dve.wait_ge(s["prep_columns"], 1)
            link(dve.tensor_copy(wide["0"][:, :, D:DX], ps[:, 4, 0:4].rearrange("p (c o) -> p c o", c=C)))
            link(dve.tensor_copy(wide["3"][:, :, D:DX], ps[:, 4, 4:8].rearrange("p (c o) -> p c o", c=C)))
            link(dve.tensor_scalar(tt_bias1[:], ps[:, 4, 8:10], D ** -0.5, None, ALU.mult))
            link(dve.tensor_copy(wide["1c"][:, :, D], ps[:, 4, 10:12]))
            dve.wait_ge(s["prep_products"], 2)
            link(dve.tensor_copy(wide["1m"][:, :, 0:D], ps[:, 5, :].rearrange("p (c n) -> p c n", c=C)))
            dve.wait_ge(s["prep_copied"], 1)
            for n in wide:
                width = D if n in ("1m", "2q", "2k") else DX
                link(dve.tensor_copy(whi[n][:, :, 0:width], wide[n][:, :, 0:width]))
                last = dve.tensor_tensor(wlo[n][:, :, 0:width], wide[n][:, :, 0:width],
                                         whi[n][:, :, 0:width].bitcast(F32), ALU.subtract)
            last.then_inc(s["prep_done"], 1)
            dve.wait_ge(s["prep_done"], 1)

            def lo_part(n, bank, hi_done, step, lag):
                if not step.runs(lag):
                    return
                ready(dve, hi_done, step, lag)
                dve.tensor_tensor(xlo[n][:].rearrange("p c g n -> p (c g n)"), ps[:, bank, :],
                                  xhi[n][:].rearrange("p c g n -> p (c g n)").bitcast(F32), ALU.subtract)\
                   .then_inc(drained[f"xt{n}"], 1)

            def attention_columns(n, name, banks, step, lag):
                if not step.runs(lag):
                    return
                ready(dve, made[name], step, lag)
                read_out(dve, made[f"kb{n}"], step, lag)
                dve.tensor_tensor(qk[n][:], ps[:, banks[0]:banks[1] + 1, D:DX], qk_const[n][:], ALU.add)\
                   .then_inc(s["qk0"] if n == 0 else s["qk3"], 1)

            def row_term1(step):
                if not step.runs(L1):
                    return
                ready(dve, made["xc1"], step, L1)
                dve.tensor_scalar(row1[:], ps[:, 4:6, D], D ** -0.5, row_const1[:, 0:1], ALU.mult, ALU.add)\
                   .then_inc(s["row1"], 1)

            def gate_columns2(step):
                if not step.runs(L2A):
                    return
                ready(dve, made["v2"], step, L2A)
                read_out(dve, made["cb2"], step, L2A)
                dve.tensor_copy(ac2[:], ps[:, 3:5, D:DX]).then_inc(s["ac2"], 1)

            def leaky_softmax_inputs(n, bank, mask_done, mask, qk_done, leaky_done, max_done, exp_done, step, lag):
                if not step.runs(lag):
                    return
                ready(dve, made[f"kb{n}"], step, lag)
                ready(dve, qk_done, step, lag)
                ready(dve, mask_done, step, lag if n == 0 else lag)
                for g in range(G):
                    last = dve.scalar_tensor_tensor(out=z[n][:, g, :], in0=ps[:, bank, g * P:(g + 1) * P],
                                                    scalar=qk[n][:, g, 0:1], in1=mask[:, g, :],
                                                    op0=ALU.add, op1=ALU.add)
                last.then_inc(drained[f"kb{n}"], 1)
                ready(dve, drained[f"kb{n}"], step, lag)
                read_out(dve, exp_done, step, lag)
                dve.scalar_tensor_tensor(out=flat(lk[n][:]), in0=flat(z[n][:]), scalar=SLOPE, in1=flat(z[n][:]),
                                         op0=ALU.mult, op1=ALU.max).then_inc(leaky_done, 1)
                ready(dve, leaky_done, step, lag)
                dve.tensor_reduce(nmax[n][:], lk[n][:], AX_X, ALU.max, negate=True).then_inc(max_done, 1)

            def masked_softmax_inputs1(step):
                if not step.runs(L1):
                    return
                ready(dve, made["s1"], step, L1)
                ready(dve, s["row1"], step, L1)
                ready(dve, s["neg1"], step, L1)
                read_out(dve, s["exp1"], step, L1)
                for g in range(G):
                    last = dve.scalar_tensor_tensor(out=z[1][:, g, :], in0=ps[:, 2, g * P:(g + 1) * P],
                                                    scalar=row1[:, g:g + 1], in1=neg[1][:, g, :],
                                                    op0=ALU.add, op1=ALU.add)
                last.then_inc(drained["s1"], 1)
                ready(dve, drained["s1"], step, L1)
                dve.tensor_reduce(nmax[1][:], z[1][:], AX_X, ALU.max, negate=True).then_inc(s["max1"], 1)
                ready(dve, s["max1"], step, L1)
                dve.tensor_scalar(flag1[:], nmax[1][:], -0.5 * NEG_MASK, None, ALU.is_lt).then_inc(s["flag1"], 1)

            def normalised_sum(n, bank, exp_done, rinv_done, xb_done, dst, step, lag):
                if not step.runs(lag):
                    return
                ready(dve, exp_done, step, lag)
                dve.reciprocal(rinv[n][:], rsum[n][:]).then_inc(rinv_done, 1)
                ready(dve, made[f"pv{n}"], step, lag)
                ready(dve, rinv_done, step, lag)
                ready(dve, xb_done, step, lag)
                if n == 0:
                    read_out(dve, made["xt1"], step, lag, halves=2)
                else:
                    moved(dve, y_stored, step, lag, before=1)
                for g in range(G):
                    last = dve.scalar_tensor_tensor(out=dst[:, g, :], in0=ps[:, bank, g * D:(g + 1) * D],
                                                    scalar=rinv[n][:, g:g + 1], in1=xb[n][:, g, :],
                                                    op0=ALU.mult, op1=ALU.add)
                last.then_inc(drained[f"pv{n}"], 1)

            def layer_norm_statistics1(step):
                if not step.runs(L1):
                    return
                ready(dve, s["exp1"], step, L1)
                dve.reciprocal(rinv[1][:], rsum[1][:]).then_inc(s["rinv1"], 1)
                ready(dve, s["rinv1"], step, L1)
                ready(dve, s["flag1"], step, L1)
                dve.tensor_tensor(rflag1[:], rinv[1][:], flag1[:], ALU.mult).then_inc(s["rflag1"], 1)
                ready(dve, s["rflag1"], step, L1)
                ready(dve, made["pv1"], step, L1)
                for g in range(G):
                    last = dve.scalar_tensor_tensor(out=sum1[:, g, :], in0=ps[:, 6, g * D:(g + 1) * D],
                                                    scalar=rflag1[:, g:g + 1], in1=x1[:, step.half(L1), g, :],
                                                    op0=ALU.mult, op1=ALU.add)
                last.then_inc(drained["pv1"], 1)
                ready(dve, drained["pv1"], step, L1)
                for g in range(G):
                    last = dve.bn_stats(stats1[:, g, :], sum1[:, g, :])
                last.then_inc(s["stats1"], 1)
                ready(dve, s["stats1"], step, L1)
                after_setup(dve)
                for g in range(G):
                    last = dve.bn_aggr(mean1[:, g, :], stats1[:, g, :])
                last.then_inc(s["mean1"], 1)
                ready(dve, s["mean1"], step, L1)
                dve.tensor_scalar(veps1[:], mean1[:, :, 1], LN_EPS, None, ALU.add).then_inc(s["veps1"], 1)

            def layer_norm1(step):
                if not step.runs(L1):
                    return
                ready(dve, s["rstd1"], step, L1)
                read_out(dve, s["gamma1"], step, L1)
                for g in range(G):
                    last = dve.tensor_scalar(norm1[:, g, :], sum1[:, g, :], mean1[:, g, 0:1], rstd1[:, g:g + 1],
                                             ALU.subtract, ALU.mult)
                last.then_inc(s["norm1"], 1)

            def scores_and_minima2(j, step):
                if not step.runs(L2B):
                    return
                ready(dve, made[f"sc{j}"], step, L2B)
                ready(dve, s["pair_bias2"], step, L2B)
                read_out(dve, (s["exp2_0"], s["exp2_1"], s["exp2_2"], s["exp2_3"])[j], step, L2B)
                after_setup(dve)
                for c in range(C):
                    for g in range(G):
                        last = dve.tensor_tensor_reduce(
                            t2[:, j, c, g, :], ps[:, j % 2, (c * G + g) * P:(c * G + g + 1) * P],
                            pair_bias2[:, g, :], -1.0, HUGE, ALU.add, ALU.min, nmax2[:, j, c, g:g + 1])
                last.then_inc(drained[f"sc{j}"], 1)

            def weights2(j, step):
                if not step.runs(L2B):
                    return
                ready(dve, made[f"pt2_{j}"], step, L2B)
                ready(dve, drained["cb2"], step, L2B)
                read_out(dve, made["pv2_1"], step, L2B)
                dve.tensor_tensor(ptm2[:, j], ps[:, j % 2, :].rearrange("p (c g n) -> p c g n", c=C, g=G),
                                  adjt2[:].rearrange("p (o g) n -> p o g n", o=1).broadcast_to([P, C, G, P]),
                                  ALU.mult).then_inc(drained[f"pt2_{j}"], 1)

            def normalised_heads2(g, step):
                if not step.runs(L2B):
                    return
                bank, rinv_done = ((5, s["rinv2_0"]), (7, s["rinv2_1"]))[g]
                heads = ps[:, bank, 0:H * (HD + 1)].rearrange("p (h d) -> p h d", h=H)
                ready(dve, made[f"pv2_{g}"], step, L2B)
                dve.reciprocal(rinv2[:, g, :], heads[:, :, HD]).then_inc(rinv_done, 1)
                ready(dve, rinv_done, step, L2B)
                read_out(dve, s["x3_ready"], step, L2B)
                dve.tensor_tensor(o2[:, g, :].rearrange("p (h d) -> p h d", h=H), heads[:, :, 0:HD],
                                  rinv2[:, g, :].rearrange("p (h o) -> p h o", o=1).broadcast_to([P, H, HD]),
                                  ALU.mult).then_inc(drained[f"pv2_{g}"], 1)

            def pair_bias_and_adjacency2(step):
                if not step.runs(L2A):
                    return
                ready(dve, made["cb2"], step, L2A)
                for g in range(G):
                    last = dve.tensor_scalar(pair_bias2[:, g, :], ps[:, 0, g * P:(g + 1) * P], ac2[:, g, 0:1],
                                             one["b_g2"][:, 0:1], ALU.add, ALU.add)
                last.then_inc(s["pair_bias2"], 1)
                dve.tensor_scalar(flat(adjt2[:]), ps[:, 0, G * P:2 * G * P], ADJ_EPS, None, ALU.add)\
                   .then_inc(drained["cb2"], 1)

            def one_step(step):
                scores_and_minima2(0, step)
                lo_part(0, 2, s["hi0"], step, L0)
                lo_part(1, 3, s["hi1"], step, L1)
                scores_and_minima2(1, step)
                lo_part(3, 4, s["hi3"], step, L3)
                lo_part(2, 5, s["hi2"], step, L2A)
                attention_columns(0, "p0", (6, 7), step, L0)
                scores_and_minima2(2, step)
                scores_and_minima2(3, step)
                leaky_softmax_inputs(0, 3, s["neg0"], neg[0], s["qk0"], s["leaky0"], s["max0"], s["exp0"], step, L0)
                row_term1(step)
                attention_columns(3, "p3", (6, 7), step, L3)
                weights2(0, step)
                masked_softmax_inputs1(step)
                weights2(1, step)
                leaky_softmax_inputs(3, 3, s["neg3"], neg[3][:, step.half(L3)], s["qk3"], s["leaky3"], s["max3"], s["exp3"],
                                     step, L3)
                weights2(2, step)
                normalised_sum(0, 7, s["exp0"], s["rinv0"], s["xb0"], x1[:, step.half(L0)], step, L0)
                weights2(3, step)
                gate_columns2(step)
                normalised_heads2(0, step)
                layer_norm_statistics1(step)
                normalised_heads2(1, step)
                layer_norm1(step)
                pair_bias_and_adjacency2(step)
                normalised_sum(3, 2, s["exp3"], s["rinv3"], s["xb3"], y[:, step.half(L3)], step, L3)

            pipeline(dve, one_step)

        @block.gpsimd
        def _(pool):
            pool.memset(minus_half[:], -0.5)
            pool.memset(v2[:, :, :, :, HD:HD + 1].rearrange("p k g h o -> p (k g h) o"), 1.0).then_inc(s["fills_done"], 1)
            pool.wait_ge(s["fills_done"], 1)
            pool.wait_ge(s["const_loaded"], 16 * n_loads[0])

            def both(row):
                return rows[row][:].rearrange("p (o d) -> p o d", o=1).broadcast_to([P, G, D])

            def leaky_mask(dst, src, mask_done):
                pool.tensor_scalar(flat(dst), flat(src), -1.0, -NEG_LEAKY, ALU.add, ALU.mult).then_inc(mask_done, 1)

            def masks(step):
                if step.runs(L2B):
                    ready(pool, s["adj1"], step, L2B)
                    read_out(pool, drained["kb3"], step, L2B, halves=2)
                    after_setup(pool)
                    leaky_mask(neg[3][:, step.half(L2B)], adj1[:, step.half(L2B)], s["neg3"])
                if step.runs(L1):
                    moved(pool, adj_loaded, step, L1)
                    read_out(pool, made["cb2"], step, L1, halves=2)
                    read_out(pool, s["neg3"], step, L1, halves=2)
                    after_setup(pool)
                    pool.tensor_scalar(flat(adj1[:, step.half(L1)]), flat(adj0[:, step.half(L1)]), 1.0, None,
                                       ALU.mult).then_inc(s["adj1"], 1)
                    read_out(pool, drained["s1"], step, L1)
                    after_setup(pool)
                    pool.tensor_scalar(flat(neg[1][:]), flat(adj0[:, step.half(L1)]), 0.0, NEG_MASK,
                                       ALU.is_equal, ALU.mult).then_inc(s["neg1"], 1)
                if step.runs(L0):
                    moved(pool, adj_loaded, step, L0)
                    read_out(pool, drained["kb0"], step, L0)
                    after_setup(pool)
                    leaky_mask(neg[0][:], adj0[:, step.half(L0)], s["neg0"])

            def input_plus_bias(dst, src, row, src_done, sum_done, readers, step, lag):
                if not step.runs(lag):
                    return
                if lag == L0:
                    moved(pool, x_loaded, step, lag)
                else:
                    ready(pool, src_done, step, lag)
                for reader, halves in readers:
                    read_out(pool, reader, step, lag, halves)
                pool.tensor_tensor(dst, src, both(row), ALU.add).then_inc(sum_done, 1)

            def full_transposed1(step):
                if not step.runs(L1):
                    return
                ready(pool, drained["xt1"], step, L1)
                read_out(pool, made["s1"], step, L1)
                pool.tensor_tensor(xt1[:].rearrange("p c g n -> p (c g n)"),
                                   xhi[1][:].rearrange("p c g n -> p (c g n)").bitcast(F32),
                                   xlo[1][:].rearrange("p c g n -> p (c g n)").bitcast(F32),
                                   ALU.add).then_inc(s["full1"], 1)

            def inverse_deviation1(step):
                if not step.runs(L1):
                    return
                ready(pool, s["veps1"], step, L1)
                pool.tensor_tensor(rstd1[:], veps1[:], minus_half[:], ALU.pow).then_inc(s["rstd1"], 1)

            def scale_and_shift1(step):
                if not step.runs(L1):
                    return
                ready(pool, s["norm1"], step, L1)
                pool.tensor_tensor(gam1[:], norm1[:], both("gamma"), ALU.mult).then_inc(s["gamma1"], 1)
                ready(pool, s["gamma1"], step, L1)
                read_out(pool, made["xt2"], step, L1)
                read_out(pool, s["xb2"], step, L1)
                pool.tensor_tensor(x2[:], gam1[:], both("beta"), ALU.add).then_inc(s["x2_ready"], 1)

            def residual2(step):
                if not step.runs(L2B):
                    return
                ready(pool, drained["pv2_0"], step, L2B)
                ready(pool, drained["pv2_1"], step, L2B)
                ready(pool, s["xb2"], step, L2B)
                read_out(pool, made["xt3"], step, L2B)
                read_out(pool, s["xb3"], step, L2B)
                pool.tensor_tensor(x3[:], o2[:], x2b[:, step.half(L2B)], ALU.add).then_inc(s["x3_ready"], 1)

            def one_step(step):
                masks(step)
                input_plus_bias(xb[0][:], x0[:, step.half(L0)], "fc_b0", None, s["xb0"],
                                [(drained["pv0"], 1)], step, L0)
                full_transposed1(step)
                input_plus_bias(xb[3][:], x3[:], "b_fc3", s["x3_ready"], s["xb3"], [(drained["pv3"], 1)], step, L3)
                input_plus_bias(x2b[:, step.half(L2A)], x2[:], "bv2", s["x2_ready"], s["xb2"],
                                [(s["x3_ready"], 2)], step, L2A)
                inverse_deviation1(step)
                scale_and_shift1(step)
                residual2(step)

            pipeline(pool, one_step)


INPUTS = ["x", "adj", "L0_gnn_fc_w", "L0_gnn_fc_b", "L0_gnn_q_w", "L0_gnn_q_b", "L0_gnn_k_w", "L0_gnn_k_b",
          "L1_gnn_Wq", "L1_gnn_bq", "L1_gnn_Wk", "L1_gnn_bk", "L1_gnn_Wc", "L1_gnn_gamma", "L1_gnn_beta",
          "L2_gnn_W_q", "L2_gnn_b_q", "L2_gnn_W_k", "L2_gnn_b_k", "L2_gnn_W_v", "L2_gnn_b_v", "L2_gnn_w_g",
          "L2_gnn_b_g", "L3_gnn_W_fc", "L3_gnn_b_fc", "L3_gnn_w_q", "L3_gnn_b_q", "L3_gnn_w_k", "L3_gnn_b_k"]
VECTORS = ("q_w", "k_w", "w_q", "w_k", "b_g")


def kernel(**inputs):
    import numpy as np
    import concourse.bacc as bacc
    from concourse.bass_utils import run_bass_kernel_spmd

    nc = bacc.Bacc("TRN2", target_bir_lowering=False, num_devices=1)
    arrays, ins = {}, {}
    for name in INPUTS:
        a = np.ascontiguousarray(inputs[name])
        if name.endswith(VECTORS):
            a = a.reshape(-1)
        arrays[f"in_{name}"] = a
    arrays["in_ident"] = np.eye(P, dtype=np.float32)
    for name, a in arrays.items():
        ins[name[3:]] = nc.dram_tensor(name, a.shape, mybir.dt.from_np(a.dtype), kind="ExternalInput").ap()
    shape = arrays["in_x"].shape
    out = nc.dram_tensor("out", shape, F32, kind="ExternalOutput").ap()
    build_program(nc, ins, out)
    result = run_bass_kernel_spmd(nc, [arrays], core_ids=[0])
    return result.results[0]["out"]
```

```python
from contextlib import ExitStack

import concourse.bass as bass
from concourse import mybir

ALU = mybir.AluOpType
ACT = mybir.ActivationFunctionType
AX_X = mybir.AxisListType.X
F32 = mybir.dt.float32
F32R = mybir.dt.float32r

P = 128
G = 2
D = 256
C = D // P
H = 8
HD = D // H
QUADS = P // HD
DX = D + 2
LATER_WEIGHTS = (("2q", D), ("2k", D), ("2v", DX), ("3", DX))
NEG_LEAKY = -1.0e9
NEG_MASK = -1.0e18
SLOPE = 0.01
HUGE = 3.0e38
ROWS = ("fc_b0", "gamma", "beta", "bv2", "b_fc3")
COLUMNS = ("L0_gnn_q_w", "L0_gnn_k_w", "L3_gnn_w_q", "L3_gnn_w_k", "L1_gnn_bq", "L1_gnn_bk", "L2_gnn_b_q",
           "L2_gnn_b_k", "L0_gnn_fc_b", "L3_gnn_b_fc")
Q_W0, _, W_Q3, _, BQ1, BK1, BQ2, BK2, FC_B0, B_FC3 = range(len(COLUMNS))
SCALARS = ("L0_gnn_q_b", "L0_gnn_k_b", "L3_gnn_b_q", "L3_gnn_b_k", "L2_gnn_b_g")
Q_B0, _, B_Q3, _, B_G2 = range(len(SCALARS))
AT_QK0, AT_DOT0, AT_DOT3, AT_DOT1, AT_WQ_BK, AT_WK_BQ, AT_QK3 = range(0, 28, 4)
LN_EPS = 1e-5
ADJ_EPS = 1e-9

L0, L1, L2A, L2B, L3 = 0, 1, 2, 3, 4
LAST_LAG = L3
PEEL = 6

BANK_USERS = {
    0: [("sc0", L2B), ("tt1", L1), ("pt2_0", L2B), ("kt2", L2A), ("v2", L2A)],
    1: [("sc2", L2B), ("xc1", L1), ("pt2_1", L2B), ("v2", L2A)],
    2: [("sc1", L2B), ("xc1", L1), ("pt2_3", L2B), ("pt3", L3), ("cb2", L2A)],
    3: [("sc3", L2B), ("p3", L3), ("pv0", L0), ("pv1", L1)],
    4: [("xt1", L1), ("p0", L0), ("p3", L3), ("pt1", L1)],
    5: [("p0", L0), ("kb3", L3), ("pt2_2", L2B), ("pv2_1", L2B)],
    6: [("xt3", L3), ("s1", L1), ("qt2", L2A), ("pv2_0", L2B)],
    7: [("xt2", L2A), ("kb0", L0), ("pt0", L0), ("pv3", L3)],
}
FIRST_BANK = {name: min(bank for bank, users in BANK_USERS.items() if name in [n for n, _ in users])
              for users in BANK_USERS.values() for name, _ in users}
SPARE_BANKS = [bank for bank, users in BANK_USERS.items() if all(lag != L0 for _, lag in users)]
PRODUCTS = sorted({name for users in BANK_USERS.values() for name, _ in users})

SEMAPHORES = (
    "x_loaded0 x_loaded1 xt_loaded0 xt_loaded1 adjt_loaded0 adjt_loaded1 adj_loaded0 adj_loaded1 y_stored0 y_stored1 "
    "columns_loaded ident_loaded weight0_loaded scalars_loaded weights1_loaded weights2_loaded rows_loaded "
    "products0 hi_columns0 weight0_hi weight0_done combined1 products1 columns1 weights1_hi prep1_done "
    "weights2_hi prep2_done fills_done "
    "hi0 hi1 hi2 hi3 lo0 "
    "qk0 qk3 row1 ac2 leaky0 leaky3 max0 max1 max3 exp0 exp1 exp3 rinv0 rinv1 rinv3 xb0 xb3 xb2 "
    "full1 flag1 rflag1 stats1 mean1 veps1 rstd1 gamma1 x2_ready "
    "adjt2 exp2_0 exp2_1 exp2_2 exp2_3 rinv2_0 rinv2_1 x3_ready "
    "neg0 neg1 neg3 adj1"
).split()


def build_program(nc, ins, out):
    x_dram, adj_dram = ins["x"], ins["adj"]
    pairs = x_dram.shape[0] // G

    with ExitStack() as ctx:
        def sb(name, shape, dtype=F32):
            return ctx.enter_context(nc.sbuf_tensor(name, shape, dtype))

        s = {n: ctx.enter_context(nc.semaphore(n)) for n in SEMAPHORES}
        made = {n: ctx.enter_context(nc.semaphore(f"{n}_made")) for n in PRODUCTS}
        drained = {n: ctx.enter_context(nc.semaphore(f"{n}_drained")) for n in PRODUCTS}

        x_loaded, adj_loaded = (s["x_loaded0"], s["x_loaded1"]), (s["adj_loaded0"], s["adj_loaded1"])
        xt_loaded, adjt_loaded = (s["xt_loaded0"], s["xt_loaded1"]), (s["adjt_loaded0"], s["adjt_loaded1"])
        y_stored = (s["y_stored0"], s["y_stored1"])

        ps = ctx.enter_context(nc.psum_tensor("ps", [P, 8, 512], F32))

        ident = sb("ident", [P, P])
        wide = {n: sb(f"w_{n}", [P, C, DX]) for n in ("0", "1c", "2q", "2k", "2v", "3")}
        whi = {n: sb(f"whi_{n}", [P, C, DX], F32R) for n in ("1m", *wide)}
        wlo = {n: sb(f"wlo_{n}", [P, C, DX], F32R) for n in whi}
        rows = sb("rows", [P, len(ROWS), D])
        columns = sb("columns", [P, C, len(COLUMNS)])
        scalars = sb("scalars", [P, len(SCALARS)])
        qk_const = {n: sb(f"qk_const{n}", [P, G, 2]) for n in (0, 3)}
        gate_const2 = sb("gate_const2", [P, G, 2])
        row_const1 = sb("row_const1", [P, 1])
        tt_bias1 = sb("tt_bias1", [P, C])
        q_bias2 = sb("q_bias2", [P, C])
        minus_half = sb("minus_half", [P, G])

        x0, x1, x2b = (sb(n, [P, 2, G, D]) for n in ("x0", "x1", "x2b"))
        xt0, adjt0 = sb("xt0", [P, 2, C, G, P]), sb("adjt0", [P, 2, G, P])
        adj0, adj1 = sb("adj0", [P, 2, G, P]), sb("adj1", [P, 2, G, P])
        x2, x3, y = sb("x2", [P, G, D]), sb("x3", [P, G, D]), sb("y", [P, 2, G, D])
        neg = {0: sb("neg0_sb", [P, G, P]), 1: sb("neg1_sb", [P, G, P]), 3: sb("neg3_sb", [P, 2, G, P])}
        xhi = {n: sb(f"xhi{n}", [P, C, G, P], F32R) for n in range(4)}
        xlo = {n: sb(f"xlo{n}", [P, C, G, P], F32R) for n in range(4)}
        qk = {n: sb(f"qk_sb{n}", [P, G, 2]) for n in (0, 3)}
        fp = {n: sb(f"fp_sb{n}", [P, G, D]) for n in (0, 3)}
        xb = {n: sb(f"xb_sb{n}", [P, G, D]) for n in (0, 3)}
        lk = {n: sb(f"leaky_sb{n}", [P, G, P]) for n in (0, 3)}
        z = {n: sb(f"z_sb{n}", [P, G, P]) for n in (0, 1, 3)}
        nmax = {n: sb(f"nmax{n}", [P, G]) for n in (0, 1, 3)}
        e = {n: sb(f"e_sb{n}", [P, G, P]) for n in (0, 1, 3)}
        rsum = {n: sb(f"rsum{n}", [P, G]) for n in (0, 1, 3)}
        rinv = {n: sb(f"rinv_sb{n}", [P, G]) for n in (0, 1, 3)}
        pt = {n: sb(f"pt_sb{n}", [P, G, P]) for n in (0, 1, 3)}
        xt1 = sb("xt1_sb", [P, C, G, P])
        tt1 = sb("tt1_sb", [P, C, G, P])
        row1 = sb("row1_sb", [P, G])
        xc1 = sb("xc1_sb", [P, G, D])
        flag1, rflag1, veps1, rstd1 = (sb(f"{n}_sb", [P, G]) for n in ("flag1", "rflag1", "veps1", "rstd1"))
        sum1, gam1 = sb("sum1_sb", [P, G, D]), sb("gam1_sb", [P, G, D])
        stats1, mean1 = sb("stats1_sb", [P, G, 6]), sb("mean1_sb", [P, G, 2])
        qt2, kt2 = sb("qt2_sb", [P, C, G, P]), sb("kt2_sb", [P, C, G, P])
        ac2 = sb("ac2_sb", [P, G, 2])
        v2 = sb("v2_sb", [P, 2, G, H, HD + 1])
        pair_bias2, adjt2 = sb("pair_bias2_sb", [P, 2, G, P]), sb("adjt2_sb", [P, 2, G, P])
        t2, e2, ptm2 = (sb(n, [P, QUADS, C, G, P]) for n in ("t2_sb", "e2_sb", "ptm2_sb"))
        turned = {n: t2[:, i].rearrange("p c g n -> p c (g n)")
                  for i, n in enumerate(("fc0", "wq1_t", "wk1_t", "wfc3_t"))}
        nmax2 = sb("nmax2", [P, QUADS, C, G])
        rinv2 = sb("rinv2_sb", [P, G, H])
        o2 = sb("o2_sb", [P, G, D])

        def bank_of(name):
            return ps[:, FIRST_BANK[name], :]

        class Step:

            def __init__(self, t, count=None):
                self.t = t
                self.count = count
                self.even = None if count is None else count * 2

            def runs(self, lag):
                return self.even is not None or 0 <= self.t - lag < pairs

            def half(self, lag):
                return (self.t - lag) % 2

            def pair(self, lag):
                return self.t - lag if self.even is None else self.even + (self.t - lag)

            def turn(self, lag):
                return (self.t - lag) // 2 if self.count is None else self.count + (self.t - lag) // 2

        def moved(eng, sems, step, lag, before=0):
            if step.count is not None or step.turn(lag) - before >= 0:
                eng.wait_ge(sems[step.half(lag)], (step.turn(lag) + (1 - before)) * 16)

        def ready(eng, sem, step, lag):
            eng.wait_ge(sem, step.pair(lag) + 1)

        def read_out(eng, sem, step, lag, halves=1):
            if step.even is not None or step.pair(lag) + 1 - halves > 0:
                eng.wait_ge(sem, step.pair(lag) + (1 - halves))

        def take_bank(eng, bank, name, step):
            users = BANK_USERS[bank]
            at = [n for n, _ in users].index(name)
            before = users[:at][::-1]
            for back in range(LAST_LAG + 2):
                for who, lag in before:
                    if step.even is not None:
                        eng.wait_ge(drained[who], step.even + (step.t - back - lag + 1))
                        return
                    if 0 <= step.t - back - lag < pairs:
                        eng.wait_ge(drained[who], step.t - back - lag + 1)
                        return
                before = users[::-1]

        def after_setup(eng):
            eng.nop(nofuse=True)

        def pipeline(eng, one_step):
            for t in range(PEEL):
                one_step(Step(t))
            with eng.Fori(PEEL // 2, pairs // 2) as i:
                for u in range(2):
                    one_step(Step(u, i))
            for t in range(pairs, pairs + LAST_LAG):
                one_step(Step(t))

        def graphs(dram, pair):
            rows_ = slice(pair * G, (pair + 1) * G) if isinstance(pair, int) else bass.ds(pair * G, G)
            return dram[rows_].rearrange("g n d -> n g d")

        def flat(ap):
            return ap.rearrange("p a b -> p (a b)")

        def flat4(ap):
            return ap.rearrange("p c g n -> p (c g n)")

        block = ctx.enter_context(nc.Block())

        @block.sync
        def _(sp):
            def load_x(pair, half):
                sp.dma_start(x0[:, half], graphs(x_dram, pair)).then_inc(x_loaded[half], 16)

            def load_turned(dst, name, loaded, pair, half):
                at = slice(pair, pair + 1) if isinstance(pair, int) else bass.ds(pair, 1)
                sp.dma_start(dst[:, half], ins[name][at].rearrange("o p w -> p (o w)")).then_inc(loaded[half], 16)

            def load_xt(pair, half):
                load_turned(xt0[:].rearrange("p h c g n -> p h (c g n)"), "x_turned", xt_loaded, pair, half)

            def load_adjt(pair, half):
                load_turned(adjt0[:].rearrange("p h g n -> p h (g n)"), "adj_turned", adjt_loaded, pair, half)

            def load_adj(pair, half):
                sp.dma_start(adj0[:, half], graphs(adj_dram, pair)).then_inc(adj_loaded[half], 16)

            def load_weight(dst, name, loaded):
                sp.dma_start(dst, ins[name].rearrange("(c p) n -> p c n", p=P)).then_inc(loaded, 16)

            load_weight(turned["fc0"], "L0_gnn_fc_w", s["columns_loaded"])
            sp.dma_start(columns[:], ins["columns"]).then_inc(s["columns_loaded"], 16)
            sp.dma_start(ident[:], ins["ident"]).then_inc(s["ident_loaded"], 16)
            load_xt(0, 0)
            load_weight(wide["0"][:, :, 0:D], "fc_w0_t", s["weight0_loaded"])
            sp.dma_start(scalars[:], ins["scalars"].broadcast_to([P, len(SCALARS)])).then_inc(s["scalars_loaded"], 16)
            load_adj(0, 0)
            load_x(0, 0)
            load_weight(turned["wq1_t"], "Wq1_t", s["weights1_loaded"])
            load_weight(turned["wk1_t"], "Wk1_t", s["weights1_loaded"])
            load_weight(turned["wfc3_t"], "W_fc3_t", s["weights1_loaded"])
            load_weight(wide["1c"][:, :, 0:D], "L1_gnn_Wc", s["weights1_loaded"])
            load_weight(wide["3"][:, :, 0:D], "L3_gnn_W_fc", s["weights1_loaded"])
            sp.dma_start(flat(rows[:]), ins["rows"].broadcast_to([P, len(ROWS) * D])).then_inc(s["rows_loaded"], 16)
            load_xt(1, 1)
            load_x(1, 1)
            load_adj(1, 1)
            load_weight(wide["2q"][:, :, 0:D], "L2_gnn_W_q", s["weights2_loaded"])
            load_weight(wide["2k"][:, :, 0:D], "L2_gnn_W_k", s["weights2_loaded"])
            load_weight(wide["2v"][:], "W_v_and_gate", s["weights2_loaded"])
            load_adjt(0, 0)
            load_adjt(1, 1)

            def one_step(step):
                if step.even is not None or step.t + 2 < pairs:
                    ready(sp, s["lo0"], step, L0)
                    load_xt(step.pair(L0 - 2), step.half(L0))
                    ready(sp, s["xb0"], step, L0)
                    load_x(step.pair(L0 - 2), step.half(L0))
                if step.runs(L1) and (step.even is not None or step.t + 1 < pairs):
                    ready(sp, s["neg1"], step, L1)
                    ready(sp, s["adj1"], step, L1)
                    load_adj(step.pair(L0 - 1), step.half(L1))
                if step.runs(L2A) and step.runs(L0):
                    ready(sp, s["adjt2"], step, L2A)
                    load_adjt(step.pair(L0), step.half(L0))
                if step.runs(L3):
                    ready(sp, drained["pv3"], step, L3)
                    sp.dma_start(graphs(out, step.pair(L3)), y[:, step.half(L3)])\
                      .then_inc(y_stored[step.half(L3)], 16)

            for t in range(PEEL):
                one_step(Step(t))
            with sp.Fori(PEEL // 2, pairs // 2 - 1) as i:
                for u in range(2):
                    one_step(Step(u, i))
            for t in range(pairs - 2, pairs + LAST_LAG):
                one_step(Step(t))
            for half in range(2):
                sp.wait_ge(y_stored[half], 16 * pairs // 2)

        @block.tensor
        def _(pe):
            def weight_products(at, weight, first, count):
                for c in range(C):
                    for k in range(C):
                        last = pe.matmul(ps[:, SPARE_BANKS[1], at + c * count:at + (c + 1) * count],
                                         weight[:, k, c * P:(c + 1) * P], columns[:, k, first:first + count],
                                         start=(k == 0), stop=(k == C - 1))
                return last

            def dot_products(at, vector, first, count):
                for k in range(C):
                    last = pe.matmul(ps[:, SPARE_BANKS[1], at:at + count],
                                     columns[:, k, vector:vector + 1].broadcast_to([P, P]),
                                     columns[:, k, first:first + count], start=(k == 0), stop=(k == C - 1))
                return last

            pe.wait_ge(s["columns_loaded"], 2 * 16)
            weight_products(AT_QK0, turned["fc0"], Q_W0, 2)
            dot_products(AT_DOT0, FC_B0, Q_W0, 2).then_inc(s["products0"], 1)
            pe.wait_ge(s["ident_loaded"], 16)

            def prepare_weights(step):
                if step.count is not None or step.t != 0:
                    return
                pe.wait_ge(s["weights1_loaded"], 5 * 16)
                dot_products(AT_DOT3, B_FC3, W_Q3, 2)
                dot_products(AT_DOT1, BQ1, BK1, 1)
                weight_products(AT_WQ_BK, turned["wq1_t"], BK1, 1)
                weight_products(AT_WK_BQ, turned["wk1_t"], BQ1, 1)
                weight_products(AT_QK3, turned["wfc3_t"], W_Q3, 2).then_inc(s["products1"], 1)

            def combine_weights(step):
                if step.count is not None or step.t != 0:
                    return
                pe.wait_ge(s["weights1_loaded"], 5 * 16)
                for c in range(C):
                    for k in range(C):
                        last = pe.matmul(ps[:, SPARE_BANKS[0], c * D:(c + 1) * D],
                                         turned["wq1_t"][:, k, c * P:(c + 1) * P], turned["wk1_t"][:, k, :],
                                         start=(k == 0), stop=(k == C - 1))
                last.then_inc(s["combined1"], 1)

            def after_preparation(step):
                if step.count is None and step.t == 1:
                    pe.wait_ge(s["prep1_done"], 1)

            def split_products(dst, left, right):
                terms = [(a, b, c) for a, b in ((0, 0), (0, 1), (1, 0)) for c in range(C)]
                for n, (a, b, c) in enumerate(terms):
                    last = pe.matmul(dst, left(a, c), right(b, c), start=(n == 0), stop=(n == len(terms) - 1))
                return last

            def x_transposes(n, src, step, lag, sem):
                if not step.runs(lag):
                    return
                ready(pe, sem, step, lag)
                bank = FIRST_BANK[f"xt{n}"]
                take_bank(pe, bank, f"xt{n}", step)
                for c in range(C):
                    for g in range(G):
                        last = pe.transpose(ps[:, bank, (c * G + g) * P:(c * G + g + 1) * P],
                                            src[:, g, c * P:(c + 1) * P], ident[:])
                last.then_inc(made[f"xt{n}"], 1)

            def node_projection(name, n, weight, step, lag, graphs_=range(G)):
                if not step.runs(lag):
                    return
                ready(pe, s["lo0"] if n == 0 else drained[f"xt{n}"], step, lag)
                if name == "p0" and step.count is None and step.t == 0:
                    pe.wait_ge(s["weight0_done"], 1)
                for g in graphs_:
                    take_bank(pe, FIRST_BANK[name] + g, name, step)
                for g in graphs_:
                    last = split_products(
                        ps[:, FIRST_BANK[name] + g, 0:DX],
                        lambda a, c: (xhi, xlo)[a][n][:, c, g, :],
                        lambda b, c: (whi, wlo)[b][weight][:, c, :])
                if G - 1 in graphs_:
                    last.then_inc(made[name], 1)

            def feature_projection(name, n, weight, step, lag):
                if not step.runs(lag):
                    return
                ready(pe, drained[f"xt{n}"], step, lag)
                if name == "qt2" and step.count is None and step.t == L2A:
                    pe.wait_ge(s["prep2_done"], 1)
                    pe.wait_ge(s["fills_done"], 1)
                bank = FIRST_BANK[name]
                take_bank(pe, bank, name, step)
                for m in range(C):
                    last = split_products(
                        ps[:, bank, m * G * P:(m + 1) * G * P],
                        lambda a, c: (whi, wlo)[a][weight][:, c, m * P:(m + 1) * P],
                        lambda b, c: flat((xhi, xlo)[b][n][:, c]))
                last.then_inc(made[name], 1)

            def key_rows(n, step, lag):
                if not step.runs(lag):
                    return
                sem = s["qk0"] if n == 0 else s["qk3"]
                ready(pe, sem, step, lag)
                bank = FIRST_BANK[f"kb{n}"]
                take_bank(pe, bank, f"kb{n}", step)
                for g in range(G):
                    last = pe.transpose(ps[:, bank, g * P:(g + 1) * P],
                                        qk[n][:, g, 1:2].broadcast_to([P, P]), ident[:])
                last.then_inc(made[f"kb{n}"], 1)

            def prob_transposes(n, exp_done, step, lag):
                if not step.runs(lag):
                    return
                ready(pe, exp_done, step, lag)
                bank = FIRST_BANK[f"pt{n}"]
                take_bank(pe, bank, f"pt{n}", step)
                for g in range(G):
                    last = pe.transpose(ps[:, bank, g * P:(g + 1) * P], e[n][:, g, :], ident[:])
                last.then_inc(made[f"pt{n}"], 1)

            def weighted_sum(n, values, copied, step, lag):
                if not step.runs(lag):
                    return
                ready(pe, drained[f"pt{n}"], step, lag)
                ready(pe, copied, step, lag)
                bank = FIRST_BANK[f"pv{n}"]
                take_bank(pe, bank, f"pv{n}", step)
                for g in range(G):
                    last = pe.matmul(ps[:, bank, g * D:(g + 1) * D], pt[n][:, g, :], values[:, g, :],
                                     start=True, stop=True)
                last.then_inc(made[f"pv{n}"], 1)

            def scores1(step):
                if not step.runs(L1):
                    return
                ready(pe, drained["tt1"], step, L1)
                ready(pe, s["full1"], step, L1)
                bank = FIRST_BANK["s1"]
                take_bank(pe, bank, "s1", step)
                for g in range(G):
                    for c in range(C):
                        last = pe.matmul(ps[:, bank, g * P:(g + 1) * P], tt1[:, c, g, :], xt1[:, c, g, :],
                                         start=(c == 0), stop=(c == C - 1))
                last.then_inc(made["s1"], 1)

            def scores2(quads, step):
                if not step.runs(L2B):
                    return
                if quads[0] == 0:
                    ready(pe, drained["qt2"], step, L2B)
                    ready(pe, drained["kt2"], step, L2B)
                for j in quads:
                    take_bank(pe, FIRST_BANK[f"sc{j}"], f"sc{j}", step)
                for c in range(C):
                    for g in range(G):
                        for j in quads:
                            rows_of = slice(j * HD, (j + 1) * HD)
                            mm = pe.matmul(ps[:, FIRST_BANK[f"sc{j}"], (c * G + g) * P:(c * G + g + 1) * P],
                                           qt2[rows_of, c, g, :], kt2[rows_of, c, g, :], start=True, stop=True)
                            if (c, g) == (C - 1, G - 1):
                                mm.then_inc(made[f"sc{j}"], 1)

            def prob_transposes2(j, step):
                if not step.runs(L2B):
                    return
                exp_done = (s["exp2_0"], s["exp2_1"], s["exp2_2"], s["exp2_3"])[j]
                ready(pe, exp_done, step, L2B)
                bank = FIRST_BANK[f"pt2_{j}"]
                take_bank(pe, bank, f"pt2_{j}", step)
                for c in range(C):
                    for g in range(G):
                        last = pe.transpose(ps[:, bank, (c * G + g) * P:(c * G + g + 1) * P],
                                            e2[:, j, c, g, :], ident[:])
                last.then_inc(made[f"pt2_{j}"], 1)

            def weighted_sum2(g, part, step):
                if not step.runs(L2B):
                    return
                bank = FIRST_BANK[f"pv2_{g}"]
                if part == 0:
                    ready(pe, drained["v2"], step, L2B)
                    take_bank(pe, bank, f"pv2_{g}", step)
                for j in (2 * part, 2 * part + 1):
                    ready(pe, drained[f"pt2_{j}"], step, L2B)
                    for c in range(C):
                        h = c * QUADS + j
                        last = pe.matmul(ps[:, bank, h * (HD + 1):(h + 1) * (HD + 1)],
                                         ptm2[:, j, c, g, :], v2[:, step.half(L2B), g, h, :],
                                         start=True, stop=True)
                if part == 1:
                    last.then_inc(made[f"pv2_{g}"], 1)

            def spread_c2(step):
                if not step.runs(L2A):
                    return
                ready(pe, s["ac2"], step, L2A)
                bank = FIRST_BANK["cb2"]
                take_bank(pe, bank, "cb2", step)
                for g in range(G):
                    last = pe.transpose(ps[:, bank, g * P:(g + 1) * P], ac2[:, g, 1:2].broadcast_to([P, P]), ident[:])
                last.then_inc(made["cb2"], 1)

            def one_step(step):
                after_preparation(step)
                scores2((0, 1), step)
                x_transposes(1, x1[:, step.half(L1)], step, L1, drained["pv0"])
                scores2((2, 3), step)
                x_transposes(2, x2, step, L2A, s["x2_ready"])
                x_transposes(3, x3, step, L3, s["x3_ready"])
                feature_projection("tt1", 1, "1m", step, L1)
                node_projection("p0", 0, "0", step, L0)
                node_projection("xc1", 1, "1c", step, L1)
                scores1(step)
                key_rows(0, step, L0)
                node_projection("p3", 3, "3", step, L3)
                prob_transposes2(1, step)
                prob_transposes2(0, step)
                feature_projection("qt2", 2, "2q", step, L2A)
                combine_weights(step)
                key_rows(3, step, L3)
                prob_transposes(0, s["exp0"], step, L0)
                feature_projection("kt2", 2, "2k", step, L2A)
                prob_transposes2(2, step)
                prob_transposes2(3, step)
                prob_transposes(1, s["exp1"], step, L1)
                weighted_sum2(0, 0, step)
                weighted_sum(0, fp[0], drained["p0"], step, L0)
                prepare_weights(step)
                node_projection("v2", 2, "2v", step, L2A, (0,))
                node_projection("v2", 2, "2v", step, L2A, (1,))
                weighted_sum(1, xc1, drained["xc1"], step, L1)
                prob_transposes(3, s["exp3"], step, L3)
                weighted_sum2(0, 1, step)
                weighted_sum2(1, 0, step)
                spread_c2(step)
                weighted_sum2(1, 1, step)
                weighted_sum(3, fp[3], drained["p3"], step, L3)

            pipeline(pe, one_step)

        @block.scalar
        def _(act):
            def prepare_weights(step):
                if step.count is not None or step.t > 1:
                    return
                if step.t == 0:
                    act.wait_ge(s["combined1"], 1)
                    act.activation(whi["1m"][:, :, 0:D], ps[:, SPARE_BANKS[0], :].rearrange("p (c n) -> p c n", c=C),
                                   ACT.Copy).then_inc(s["weights1_hi"], 1)
                    act.wait_ge(s["columns1"], 1)
                    act.activation(whi["1c"][:], wide["1c"][:], ACT.Copy).then_inc(s["weights1_hi"], 1)
                else:
                    act.wait_ge(s["weights2_loaded"], 3 * 16)
                    for n, width in LATER_WEIGHTS:
                        act.activation(whi[n][:, :, 0:width], wide[n][:, :, 0:width], ACT.Copy)\
                           .then_inc(s["weights2_hi"], 1)

            def after_preparation(step):
                if step.count is None and step.t == 1:
                    act.wait_ge(s["prep1_done"], 1)

            def hi_part(n, step, lag, hi_done, last_reads):
                if not step.runs(lag):
                    return
                if n == 0:
                    moved(act, xt_loaded, step, lag)
                    src = flat4(xt0[:, step.half(lag)])
                else:
                    ready(act, made[f"xt{n}"], step, lag)
                    src = ps[:, FIRST_BANK[f"xt{n}"], :]
                for reader in last_reads:
                    read_out(act, reader, step, lag)
                act.activation(flat4(xhi[n][:]), src, ACT.Copy)\
                   .then_inc(hi_done, 1)

            def copy_projection(name, dst, columns_read, step, lag, last_read):
                if not step.runs(lag):
                    return
                ready(act, columns_read, step, lag)
                read_out(act, last_read, step, lag)
                act.activation(dst, ps[:, FIRST_BANK[name]:FIRST_BANK[name] + G, 0:D], ACT.Copy)\
                   .then_inc(drained[name], 1)

            def exponentials(n, max_done, exp_done, step, lag):
                if not step.runs(lag):
                    return
                ready(act, max_done, step, lag)
                read_out(act, made[f"pt{n}"], step, lag)
                src = z[1] if n == 1 else lk[n]
                for g in range(G):
                    last = act.activation(e[n][:, g, :], src[:, g, :], ACT.Exp, bias=nmax[n][:, g:g + 1],
                                          accum_out=rsum[n][:, g:g + 1])
                last.then_inc(exp_done, 1)

            def copy_probs(n, step, lag):
                if not step.runs(lag):
                    return
                ready(act, made[f"pt{n}"], step, lag)
                read_out(act, made[f"pv{n}"], step, lag)
                act.activation(flat(pt[n][:]), bank_of(f"pt{n}")[:, 0:G * P], ACT.Copy).then_inc(drained[f"pt{n}"], 1)

            def biased_copy(name, dst, scale, bias, step, lag, readers):
                if not step.runs(lag):
                    return
                ready(act, made[name], step, lag)
                for reader, reader_lag in readers:
                    read_out(act, reader, step, lag)
                for c in range(C):
                    last = act.activation(flat(dst[:, c]), ps[:, FIRST_BANK[name], c * G * P:(c + 1) * G * P],
                                          ACT.Identity, bias=bias(c), scale=scale)
                last.then_inc(drained[name], 1)

            def exponentials2(j, step):
                if not step.runs(L2B):
                    return
                ready(act, drained[f"sc{j}"], step, L2B)
                read_out(act, made[f"pt2_{j}"], step, L2B)
                for c in range(C):
                    for g in range(G):
                        last = act.activation(e2[:, j, c, g, :], t2[:, j, c, g, :], ACT.Exp, scale=-1.0,
                                              bias=nmax2[:, j, c, g:g + 1])
                last.then_inc((s["exp2_0"], s["exp2_1"], s["exp2_2"], s["exp2_3"])[j], 1)

            def pair_biases2(step):
                if not step.runs(L2A):
                    return
                ready(act, s["ac2"], step, L2A)
                ready(act, made["cb2"], step, L2A)
                read_out(act, drained["sc3"], step, L2A, halves=2)
                for g in range(G):
                    last = act.activation(pair_bias2[:, step.half(L2A), g, :], bank_of("cb2")[:, g * P:(g + 1) * P],
                                          ACT.Identity, bias=ac2[:, g, 0:1])
                last.then_inc(drained["cb2"], 1)

            def copy_v2(step):
                if not step.runs(L2A):
                    return
                ready(act, s["ac2"], step, L2A)
                read_out(act, made["pv2_1"], step, L2A, halves=2)
                for g in range(G):
                    last = act.activation(v2[:, step.half(L2A), g, :, 0:HD],
                                          ps[:, FIRST_BANK["v2"] + g, 0:D].rearrange("p (h d) -> p h d", h=H),
                                          ACT.Copy)
                last.then_inc(drained["v2"], 1)

            def one_step(step):
                after_preparation(step)
                hi_part(0, step, L0, s["hi0"], [made["p0"]])
                hi_part(1, step, L1, s["hi1"], [made["xc1"], s["full1"]])
                exponentials2(0, step)
                hi_part(3, step, L3, s["hi3"], [made["p3"]])
                biased_copy("tt1", tt1, D ** -0.5, lambda c: tt_bias1[:, c:c + 1], step, L1, [(made["s1"], L1)])
                hi_part(2, step, L2A, s["hi2"], [made["v2"]])
                exponentials2(1, step)
                copy_projection("p0", fp[0][:], s["qk0"], step, L0, made["pv0"])
                exponentials2(2, step)
                copy_projection("xc1", xc1[:], s["row1"], step, L1, made["pv1"])
                exponentials2(3, step)
                exponentials(1, s["max1"], s["exp1"], step, L1)
                exponentials(0, s["max0"], s["exp0"], step, L0)
                copy_projection("p3", fp[3][:], s["qk3"], step, L3, made["pv3"])
                copy_probs(0, step, L0)
                prepare_weights(step)
                biased_copy("qt2", qt2, HD ** -0.5, lambda c: q_bias2[:, c:c + 1], step, L2A, [(made["sc3"], L2B)])
                exponentials(3, s["max3"], s["exp3"], step, L3)
                copy_probs(1, step, L1)
                biased_copy("kt2", kt2, 1.0, lambda c: columns[:, c, BK2:BK2 + 1], step, L2A, [(made["sc3"], L2B)])
                copy_probs(3, step, L3)
                copy_v2(step)
                pair_biases2(step)

            act.wait_ge(s["weight0_loaded"], 16)
            act.activation(whi["0"][:, :, 0:D], wide["0"][:, :, 0:D], ACT.Copy).then_inc(s["weight0_hi"], 1)
            pipeline(act, one_step)

        @block.vector
        def _(dve):
            dve.wait_ge(s["scalars_loaded"], 16)
            dve.wait_ge(s["products0"], 1)
            small = ps[:, SPARE_BANKS[1], :]

            def chunks(at, count):
                return small[:, at:at + C * count].rearrange("p (c o) -> p c o", c=C)

            def logit_constants(n, at, first):
                return dve.tensor_tensor(
                    qk_const[n][:], small[:, at:at + 2].rearrange("p (g o) -> p g o", g=1).broadcast_to([P, G, 2]),
                    scalars[:, first:first + 2].rearrange("p (g o) -> p g o", g=1).broadcast_to([P, G, 2]), ALU.add)

            dve.tensor_copy(whi["0"][:, :, D:DX], chunks(AT_QK0, 2)).then_inc(s["hi_columns0"], 1)
            logit_constants(0, AT_DOT0, Q_B0)
            dve.wait_ge(s["hi_columns0"], 1)
            dve.tensor_tensor(wlo["0"][:, :, D:DX], chunks(AT_QK0, 2), whi["0"][:, :, D:DX].bitcast(F32), ALU.subtract)
            dve.wait_ge(s["weight0_hi"], 1)
            dve.tensor_tensor(wlo["0"][:, :, 0:D], wide["0"][:, :, 0:D],
                              whi["0"][:, :, 0:D].bitcast(F32), ALU.subtract).then_inc(s["weight0_done"], 1)

            def prepare_weights(step):
                if step.count is not None or step.t != 0:
                    return
                dve.wait_ge(s["weights1_hi"], 1)
                dve.tensor_tensor(wlo["1m"][:, :, 0:D], ps[:, SPARE_BANKS[0], :].rearrange("p (c n) -> p c n", c=C),
                                  whi["1m"][:, :, 0:D].bitcast(F32), ALU.subtract)
                dve.memset(wide["1c"][:, :, D + 1:DX], 0.0)
                dve.memset(gate_const2[:, :, 1], 0.0)
                dve.tensor_copy(gate_const2[:, :, 0], scalars[:, B_G2:B_G2 + 1].broadcast_to([P, G]))
                dve.tensor_scalar(q_bias2[:], columns[:, :, BQ2], HD ** -0.5, None, ALU.mult)
                dve.wait_ge(s["products1"], 1)
                dve.tensor_copy(wide["1c"][:, :, D:D + 1], chunks(AT_WQ_BK, 1))
                dve.tensor_copy(wide["3"][:, :, D:DX], chunks(AT_QK3, 2)).then_inc(s["columns1"], 1)
                dve.tensor_scalar(tt_bias1[:], small[:, AT_WK_BQ:AT_WK_BQ + C], D ** -0.5, None, ALU.mult)
                dve.tensor_scalar(row_const1[:], small[:, AT_DOT1:AT_DOT1 + 1], D ** -0.5, None, ALU.mult)
                logit_constants(3, AT_DOT3, B_Q3)
                dve.wait_ge(s["weights1_hi"], 2)
                dve.tensor_tensor(wlo["1c"][:], wide["1c"][:], whi["1c"][:].bitcast(F32), ALU.subtract)\
                   .then_inc(s["prep1_done"], 1)

            def after_preparation(step):
                if step.count is None and step.t == 0:
                    dve.wait_ge(s["weight0_done"], 1)
                if step.count is None and step.t == 1:
                    dve.wait_ge(s["prep1_done"], 1)
                    dve.wait_ge(s["rows_loaded"], 16)

            def lo_part(n, hi_done, step, lag):
                if not step.runs(lag):
                    return
                ready(dve, hi_done, step, lag)
                dve.tensor_tensor(flat4(xlo[n][:]), ps[:, FIRST_BANK[f"xt{n}"], :], flat4(xhi[n][:]).bitcast(F32),
                                  ALU.subtract)\
                   .then_inc(drained[f"xt{n}"], 1)

            def attention_columns(n, step, lag):
                if not step.runs(lag):
                    return
                bank = FIRST_BANK[f"p{n}"]
                ready(dve, made[f"p{n}"], step, lag)
                read_out(dve, made[f"kb{n}"], step, lag)
                dve.tensor_tensor(qk[n][:], ps[:, bank:bank + G, D:DX], qk_const[n][:], ALU.add)\
                   .then_inc(s["qk0"] if n == 0 else s["qk3"], 1)

            def row_term1(step):
                if not step.runs(L1):
                    return
                ready(dve, made["xc1"], step, L1)
                bank = FIRST_BANK["xc1"]
                dve.tensor_scalar(row1[:], ps[:, bank:bank + G, D], D ** -0.5, row_const1[:, 0:1], ALU.mult, ALU.add)\
                   .then_inc(s["row1"], 1)

            def gate_columns2(step):
                if not step.runs(L2A):
                    return
                ready(dve, made["v2"], step, L2A)
                read_out(dve, drained["cb2"], step, L2A)
                bank = FIRST_BANK["v2"]
                dve.tensor_tensor(ac2[:], ps[:, bank:bank + G, D:DX], gate_const2[:], ALU.add).then_inc(s["ac2"], 1)

            def leaky_softmax_inputs(n, mask_done, mask, qk_done, leaky_done, max_done, exp_done, step, lag):
                if not step.runs(lag):
                    return
                ready(dve, made[f"kb{n}"], step, lag)
                ready(dve, qk_done, step, lag)
                ready(dve, mask_done, step, lag)
                bank = FIRST_BANK[f"kb{n}"]
                for g in range(G):
                    last = dve.scalar_tensor_tensor(out=z[n][:, g, :], in0=ps[:, bank, g * P:(g + 1) * P],
                                                    scalar=qk[n][:, g, 0:1], in1=mask[:, g, :],
                                                    op0=ALU.add, op1=ALU.add)
                last.then_inc(drained[f"kb{n}"], 1)
                ready(dve, drained[f"kb{n}"], step, lag)
                read_out(dve, exp_done, step, lag)
                dve.scalar_tensor_tensor(out=flat(lk[n][:]), in0=flat(z[n][:]), scalar=SLOPE, in1=flat(z[n][:]),
                                         op0=ALU.mult, op1=ALU.max).then_inc(leaky_done, 1)
                ready(dve, leaky_done, step, lag)
                dve.tensor_reduce(nmax[n][:], lk[n][:], AX_X, ALU.max, negate=True).then_inc(max_done, 1)

            def masked_softmax_inputs1(step):
                if not step.runs(L1):
                    return
                ready(dve, made["s1"], step, L1)
                ready(dve, s["row1"], step, L1)
                ready(dve, s["neg1"], step, L1)
                read_out(dve, s["exp1"], step, L1)
                for g in range(G):
                    last = dve.scalar_tensor_tensor(out=z[1][:, g, :], in0=ps[:, FIRST_BANK["s1"], g * P:(g + 1) * P],
                                                    scalar=row1[:, g:g + 1], in1=neg[1][:, g, :],
                                                    op0=ALU.add, op1=ALU.add)
                last.then_inc(drained["s1"], 1)
                ready(dve, drained["s1"], step, L1)
                dve.tensor_reduce(nmax[1][:], z[1][:], AX_X, ALU.max, negate=True).then_inc(s["max1"], 1)
                ready(dve, s["max1"], step, L1)
                dve.tensor_scalar(flag1[:], nmax[1][:], -0.5 * NEG_MASK, None, ALU.is_lt).then_inc(s["flag1"], 1)

            def normalised_sum(n, exp_done, rinv_done, xb_done, dst, step, lag):
                if not step.runs(lag):
                    return
                ready(dve, exp_done, step, lag)
                dve.reciprocal(rinv[n][:], rsum[n][:]).then_inc(rinv_done, 1)
                ready(dve, made[f"pv{n}"], step, lag)
                ready(dve, rinv_done, step, lag)
                ready(dve, xb_done, step, lag)
                if n == 0:
                    read_out(dve, made["xt1"], step, lag, halves=2)
                else:
                    moved(dve, y_stored, step, lag, before=1)
                for g in range(G):
                    last = dve.scalar_tensor_tensor(out=dst[:, g, :], in0=bank_of(f"pv{n}")[:, g * D:(g + 1) * D],
                                                    scalar=rinv[n][:, g:g + 1], in1=xb[n][:, g, :],
                                                    op0=ALU.mult, op1=ALU.add)
                last.then_inc(drained[f"pv{n}"], 1)

            def layer_norm_statistics1(step):
                if not step.runs(L1):
                    return
                ready(dve, s["exp1"], step, L1)
                dve.reciprocal(rinv[1][:], rsum[1][:]).then_inc(s["rinv1"], 1)
                ready(dve, s["rinv1"], step, L1)
                ready(dve, s["flag1"], step, L1)
                dve.tensor_tensor(rflag1[:], rinv[1][:], flag1[:], ALU.mult).then_inc(s["rflag1"], 1)
                ready(dve, s["rflag1"], step, L1)
                ready(dve, made["pv1"], step, L1)
                for g in range(G):
                    last = dve.scalar_tensor_tensor(out=sum1[:, g, :], in0=ps[:, FIRST_BANK["pv1"], g * D:(g + 1) * D],
                                                    scalar=rflag1[:, g:g + 1], in1=x1[:, step.half(L1), g, :],
                                                    op0=ALU.mult, op1=ALU.add)
                last.then_inc(drained["pv1"], 1)
                ready(dve, drained["pv1"], step, L1)
                for g in range(G):
                    last = dve.bn_stats(stats1[:, g, :], sum1[:, g, :])
                last.then_inc(s["stats1"], 1)
                ready(dve, s["stats1"], step, L1)
                after_setup(dve)
                for g in range(G):
                    last = dve.bn_aggr(mean1[:, g, :], stats1[:, g, :])
                last.then_inc(s["mean1"], 1)
                ready(dve, s["mean1"], step, L1)
                dve.tensor_scalar(veps1[:], mean1[:, :, 1], LN_EPS, None, ALU.add).then_inc(s["veps1"], 1)

            def scaled_deviation1(step):
                if not step.runs(L1):
                    return
                ready(dve, s["mean1"], step, L1)
                for g in range(G):
                    last = dve.scalar_tensor_tensor(out=gam1[:, g, :], in0=sum1[:, g, :], scalar=mean1[:, g, 0:1],
                                                    in1=rows[:, ROWS.index("gamma"), :],
                                                    op0=ALU.subtract, op1=ALU.mult)
                last.then_inc(s["gamma1"], 1)

            def layer_norm1(step):
                if not step.runs(L1):
                    return
                ready(dve, s["rstd1"], step, L1)
                ready(dve, s["gamma1"], step, L1)
                read_out(dve, made["xt2"], step, L1)
                read_out(dve, s["xb2"], step, L1)
                for g in range(G):
                    last = dve.scalar_tensor_tensor(out=x2[:, g, :], in0=gam1[:, g, :], scalar=rstd1[:, g:g + 1],
                                                    in1=rows[:, ROWS.index("beta"), :], op0=ALU.mult, op1=ALU.add)
                last.then_inc(s["x2_ready"], 1)

            def scores_and_minima2(j, step):
                if not step.runs(L2B):
                    return
                ready(dve, made[f"sc{j}"], step, L2B)
                ready(dve, drained["cb2"], step, L2B)
                read_out(dve, (s["exp2_0"], s["exp2_1"], s["exp2_2"], s["exp2_3"])[j], step, L2B)
                after_setup(dve)
                for c in range(C):
                    for g in range(G):
                        last = dve.tensor_tensor_reduce(
                            t2[:, j, c, g, :], ps[:, FIRST_BANK[f"sc{j}"], (c * G + g) * P:(c * G + g + 1) * P],
                            pair_bias2[:, step.half(L2B), g, :], -1.0, HUGE, ALU.add, ALU.min, nmax2[:, j, c, g:g + 1])
                last.then_inc(drained[f"sc{j}"], 1)

            def weights2(j, step):
                if not step.runs(L2B):
                    return
                ready(dve, made[f"pt2_{j}"], step, L2B)
                ready(dve, s["adjt2"], step, L2B)
                read_out(dve, made["pv2_1"], step, L2B)
                adjacency = adjt2[:, step.half(L2B)].rearrange("p (o g) n -> p o g n", o=1).broadcast_to([P, C, G, P])
                dve.tensor_tensor(ptm2[:, j], bank_of(f"pt2_{j}").rearrange("p (c g n) -> p c g n", c=C, g=G),
                                  adjacency, ALU.mult).then_inc(drained[f"pt2_{j}"], 1)

            def normalised_heads2(g, step):
                if not step.runs(L2B):
                    return
                bank, rinv_done = FIRST_BANK[f"pv2_{g}"], (s["rinv2_0"], s["rinv2_1"])[g]
                heads = ps[:, bank, 0:H * (HD + 1)].rearrange("p (h d) -> p h d", h=H)
                ready(dve, made[f"pv2_{g}"], step, L2B)
                dve.reciprocal(rinv2[:, g, :], heads[:, :, HD]).then_inc(rinv_done, 1)
                ready(dve, rinv_done, step, L2B)
                read_out(dve, s["x3_ready"], step, L2B)
                dve.tensor_tensor(o2[:, g, :].rearrange("p (h d) -> p h d", h=H), heads[:, :, 0:HD],
                                  rinv2[:, g, :].rearrange("p (h o) -> p h o", o=1).broadcast_to([P, H, HD]),
                                  ALU.mult).then_inc(drained[f"pv2_{g}"], 1)

            def one_step(step):
                after_preparation(step)
                scores_and_minima2(0, step)
                lo_part(1, s["hi1"], step, L1)
                scores_and_minima2(1, step)
                scores_and_minima2(2, step)
                lo_part(3, s["hi3"], step, L3)
                scores_and_minima2(3, step)
                lo_part(2, s["hi2"], step, L2A)
                attention_columns(0, step, L0)
                row_term1(step)
                masked_softmax_inputs1(step)
                leaky_softmax_inputs(0, s["neg0"], neg[0], s["qk0"], s["leaky0"], s["max0"], s["exp0"], step, L0)
                attention_columns(3, step, L3)
                weights2(0, step)
                weights2(1, step)
                leaky_softmax_inputs(3, s["neg3"], neg[3][:, step.half(L3)], s["qk3"], s["leaky3"], s["max3"],
                                     s["exp3"], step, L3)
                weights2(2, step)
                normalised_sum(0, s["exp0"], s["rinv0"], s["xb0"], x1[:, step.half(L0)], step, L0)
                prepare_weights(step)
                weights2(3, step)
                gate_columns2(step)
                layer_norm_statistics1(step)
                normalised_heads2(0, step)
                scaled_deviation1(step)
                layer_norm1(step)
                normalised_heads2(1, step)
                normalised_sum(3, s["exp3"], s["rinv3"], s["xb3"], y[:, step.half(L3)], step, L3)

            pipeline(dve, one_step)

        @block.gpsimd
        def _(pool):
            pool.memset(minus_half[:], -0.5)
            pool.memset(v2[:, :, :, :, HD:HD + 1].rearrange("p k g h o -> p (k g h) o"), 1.0)\
                .then_inc(s["fills_done"], 1)
            pool.wait_ge(s["fills_done"], 1)

            def both(row):
                return rows[:, ROWS.index(row):ROWS.index(row) + 1, :].broadcast_to([P, G, D])

            def prepare_weights(step):
                if step.count is not None or step.t != 1:
                    return
                for i, (n, width) in enumerate(LATER_WEIGHTS):
                    pool.wait_ge(s["weights2_hi"], i + 1)
                    last = pool.tensor_tensor(wlo[n][:, :, 0:width], wide[n][:, :, 0:width],
                                              whi[n][:, :, 0:width].bitcast(F32), ALU.subtract)
                last.then_inc(s["prep2_done"], 1)

            def leaky_mask(dst, src, mask_done):
                pool.tensor_scalar(flat(dst), flat(src), -1.0, -NEG_LEAKY, ALU.add, ALU.mult).then_inc(mask_done, 1)

            def masks(step):
                if step.runs(L2B):
                    ready(pool, s["adj1"], step, L2B)
                    read_out(pool, drained["kb3"], step, L2B, halves=2)
                    after_setup(pool)
                    leaky_mask(neg[3][:, step.half(L2B)], adj1[:, step.half(L2B)], s["neg3"])
                if step.runs(L1):
                    moved(pool, adj_loaded, step, L1)
                    read_out(pool, s["neg3"], step, L1, halves=2)
                    after_setup(pool)
                    pool.tensor_scalar(flat(adj1[:, step.half(L1)]), flat(adj0[:, step.half(L1)]), 1.0, 0.0,
                                       ALU.mult, ALU.add).then_inc(s["adj1"], 1)
                    read_out(pool, drained["s1"], step, L1)
                    after_setup(pool)
                    pool.tensor_scalar(flat(neg[1][:]), flat(adj0[:, step.half(L1)]), 0.0, NEG_MASK,
                                       ALU.is_equal, ALU.mult).then_inc(s["neg1"], 1)
                if step.runs(L0):
                    moved(pool, adj_loaded, step, L0)
                    read_out(pool, drained["kb0"], step, L0)
                    after_setup(pool)
                    leaky_mask(neg[0][:], adj0[:, step.half(L0)], s["neg0"])

            def kept_adjacency2(step):
                if not step.runs(L2A):
                    return
                moved(pool, adjt_loaded, step, L2A)
                read_out(pool, drained["pt2_3"], step, L2A, halves=2)
                after_setup(pool)
                pool.tensor_scalar(flat(adjt2[:, step.half(L2A)]), flat(adjt0[:, step.half(L2A)]), ADJ_EPS, 1.0,
                                   ALU.add, ALU.mult).then_inc(s["adjt2"], 1)

            def lo_part0(step):
                if not step.runs(L0):
                    return
                ready(pool, s["hi0"], step, L0)
                read_out(pool, made["p0"], step, L0)
                pool.tensor_tensor(flat4(xlo[0][:]), flat4(xt0[:, step.half(L0)]), flat4(xhi[0][:]).bitcast(F32),
                                   ALU.subtract).then_inc(s["lo0"], 1)

            def input_plus_bias(dst, src, row, src_done, sum_done, readers, step, lag):
                if not step.runs(lag):
                    return
                if lag == L0:
                    if step.count is None and step.t == 0:
                        pool.wait_ge(s["rows_loaded"], 16)
                    moved(pool, x_loaded, step, lag)
                else:
                    ready(pool, src_done, step, lag)
                for reader, halves in readers:
                    read_out(pool, reader, step, lag, halves)
                pool.tensor_tensor(dst, src, both(row), ALU.add).then_inc(sum_done, 1)

            def full_transposed1(step):
                if not step.runs(L1):
                    return
                ready(pool, drained["xt1"], step, L1)
                read_out(pool, made["s1"], step, L1)
                pool.tensor_tensor(xt1[:].rearrange("p c g n -> p (c g n)"),
                                   xhi[1][:].rearrange("p c g n -> p (c g n)").bitcast(F32),
                                   xlo[1][:].rearrange("p c g n -> p (c g n)").bitcast(F32),
                                   ALU.add).then_inc(s["full1"], 1)

            def inverse_deviation1(step):
                if not step.runs(L1):
                    return
                ready(pool, s["veps1"], step, L1)
                pool.tensor_tensor(rstd1[:], veps1[:], minus_half[:], ALU.pow).then_inc(s["rstd1"], 1)

            def residual2(step):
                if not step.runs(L2B):
                    return
                ready(pool, drained["pv2_0"], step, L2B)
                ready(pool, drained["pv2_1"], step, L2B)
                ready(pool, s["xb2"], step, L2B)
                read_out(pool, made["xt3"], step, L2B)
                read_out(pool, s["xb3"], step, L2B)
                pool.tensor_tensor(x3[:], o2[:], x2b[:, step.half(L2B)], ALU.add).then_inc(s["x3_ready"], 1)

            def one_step(step):
                lo_part0(step)
                input_plus_bias(xb[0][:], x0[:, step.half(L0)], "fc_b0", None, s["xb0"],
                                [(drained["pv0"], 1)], step, L0)
                full_transposed1(step)
                masks(step)
                input_plus_bias(xb[3][:], x3[:], "b_fc3", s["x3_ready"], s["xb3"], [(drained["pv3"], 1)], step, L3)
                prepare_weights(step)
                kept_adjacency2(step)
                input_plus_bias(x2b[:, step.half(L2A)], x2[:], "bv2", s["x2_ready"], s["xb2"],
                                [(s["x3_ready"], 2)], step, L2A)
                inverse_deviation1(step)
                residual2(step)

            pipeline(pool, one_step)


PLAIN = ("x", "adj", "L0_gnn_fc_w", "L1_gnn_Wc", "L2_gnn_W_q", "L2_gnn_W_k", "L3_gnn_W_fc")
TURNED = {"fc_w0_t": "L0_gnn_fc_w", "Wq1_t": "L1_gnn_Wq", "Wk1_t": "L1_gnn_Wk", "W_fc3_t": "L3_gnn_W_fc"}


def layout(inputs):
    import numpy as np
    arrays = {f"in_{name}": np.ascontiguousarray(inputs[name]) for name in PLAIN}
    pairs = inputs["x"].shape[0] // G
    arrays["in_x_turned"] = np.ascontiguousarray(
        np.asarray(inputs["x"]).reshape(pairs, G, P, C, P).transpose(0, 4, 3, 1, 2)).reshape(pairs, P, -1)
    arrays["in_adj_turned"] = np.ascontiguousarray(
        np.asarray(inputs["adj"]).reshape(pairs, G, P, P).transpose(0, 3, 1, 2)).reshape(pairs, P, -1)
    for name, source in TURNED.items():
        arrays[f"in_{name}"] = np.ascontiguousarray(np.asarray(inputs[source]).T)
    vector = {name: np.asarray(a).reshape(-1) for name, a in inputs.items() if name not in PLAIN}
    arrays["in_W_v_and_gate"] = np.concatenate(
        [inputs["L2_gnn_W_v"], vector["L2_gnn_w_g"].reshape(2, D).T], axis=1)
    arrays["in_rows"] = np.concatenate(
        [vector[n] for n in ("L0_gnn_fc_b", "L1_gnn_gamma", "L1_gnn_beta", "L2_gnn_b_v", "L3_gnn_b_fc")]).reshape(1, -1)
    arrays["in_columns"] = np.ascontiguousarray(
        np.stack([vector[n].reshape(C, P) for n in COLUMNS]).transpose(2, 1, 0))
    arrays["in_scalars"] = np.concatenate([vector[n] for n in SCALARS]).reshape(1, -1)
    arrays["in_ident"] = np.eye(P, dtype=np.float32)
    return arrays


def kernel(**inputs):
    import concourse.bacc as bacc
    from concourse.bass_utils import run_bass_kernel_spmd

    nc = bacc.Bacc("TRN2", target_bir_lowering=False, num_devices=1)
    arrays, ins = layout(inputs), {}
    for name, a in arrays.items():
        ins[name[3:]] = nc.dram_tensor(name, a.shape, mybir.dt.from_np(a.dtype), kind="ExternalInput").ap()
    shape = arrays["in_x"].shape
    out = nc.dram_tensor("out", shape, F32, kind="ExternalOutput").ap()
    build_program(nc, ins, out)
    result = run_bass_kernel_spmd(nc, [arrays], core_ids=[0])
    return result.results[0]["out"]
```
